# Optimizing a Trainium2 kernel written in Bass

```python
import numpy as np
import jax
import jax.numpy as jnp

def _softmax(x, axis=-1):
    return jax.nn.softmax(x, axis=axis)

def _gelu(x):
    return jax.nn.gelu(x, approximate=True)

def _silu(x):
    return jax.nn.silu(x)

def _sigmoid(x):
    return jax.nn.sigmoid(x)

def _layernorm(x, axis=-1, eps=1e-05):
    m = jnp.mean(x, axis=axis, keepdims=True)
    v = jnp.var(x, axis=axis, keepdims=True)
    return (x - m) / jnp.sqrt(v + eps)

def _scatter_add(tgt, idx, src, axis=0):
    return tgt.at[idx].add(src)

def _segment_sum(src, seg, n):
    return jax.ops.segment_sum(src, seg, n)
kernel_name = 'mk_flamingo_gated_d1_seqx_r4_0c01fd'

def setup_inputs(seed: int=0):
    np.random.seed(seed)
    _w = jnp.asarray

    def _rec_inputs():
        import jax
        import jax.numpy as jnp
        _rk = jax.random.key(seed)
        x = -0.0005207 + 1.001 * jax.random.normal(jax.random.fold_in(_rk, 1), (16, 128, 256), jnp.float32)
        _lenS = 128 - jax.random.randint(jax.random.fold_in(_rk, 7), (16,), 0, max(1, 128 // 4) + 1, jnp.int32)
        _lenS2 = 128 - jax.random.randint(jax.random.fold_in(_rk, 8), (16,), 0, max(1, 128 // 4) + 1, jnp.int32)
        _ctx_1024P = jax.random.normal(jax.random.fold_in(_rk, 11), (16, 16, 256), jnp.float32)
        _ctx_1024c = jax.random.dirichlet(jax.random.fold_in(_rk, 511), 0.3 * jnp.ones((16,), jnp.float32), (16, 128))
        _ctx_1024t = jnp.einsum('bsk,bkd->bsd', _ctx_1024c, _ctx_1024P)
        _ctx_1024t = _ctx_1024t * jax.lax.rsqrt(jnp.mean(jnp.square(_ctx_1024t)) + 1e-12) * 0.953939
        ctx_1024 = -0.000514642 + 1.00011 * (_ctx_1024t + 0.3 * jax.random.normal(jax.random.fold_in(_rk, 611), (16, 128, 256), jnp.float32))
        _g = jax.random.normal(jax.random.fold_in(_rk, 9001), (2, 1), jnp.float32)
        _g = jnp.sign(_g) * jnp.maximum(jnp.abs(_g), 1.0) + (_g == 0) * 1.0
        g_xattn = _g[0]
        g_ffn = _g[1]
        return (x, ctx_1024, g_xattn, g_ffn)
    x, ctx_1024, g_xattn, g_ffn = _rec_inputs()

    def _L0_xattn_setup():
        import jax, jax.numpy as jnp
        import numpy as np
        B, S, E, NH = (1, 512, 256, 8)
        DH = E // NH
        EPS_BACKEND = 1e-06
        EPS_NORM = 1e-05
        key = jax.random.key(seed)
        ks = jax.random.split(key, 8)
        q = jax.random.normal(ks[0], (B, S, E), jnp.float32)
        k = jax.random.normal(ks[1], (B, S, E), jnp.float32)
        v = jax.random.normal(ks[2], (B, S, E), jnp.float32)
        igate_w = jax.random.normal(ks[3], (NH, 3 * E), jnp.float32) * 0.02
        igate_b = jax.random.normal(ks[4], (NH,), jnp.float32) * 0.1
        fgate_w = jax.random.normal(ks[5], (NH, 3 * E), jnp.float32) * 0.02
        fgate_b = jnp.linspace(3.0, 6.0, NH).astype(jnp.float32)
        norm_w = 1.0 + 0.1 * jax.random.normal(ks[6], (E,), jnp.float32)
        return dict(q=q, k=k, v=v, igate_w=igate_w, igate_b=igate_b, fgate_w=fgate_w, fgate_b=fgate_b, norm_w=norm_w)
    _L0_xattn_all = _L0_xattn_setup()
    _L0_xattn_in = {k: v for k, v in _L0_xattn_all.items() if k in ('igate_w', 'igate_b', 'fgate_w', 'fgate_b', 'norm_w')}
    del _L0_xattn_all

    def _L0_ffn_setup():
        import jax, jax.numpy as jnp
        import numpy as np
        B, T, C, E, K, CAP, H = (8, 512, 256, 8, 2, 1024, 1024)
        key = jax.random.key(seed)
        ks = jax.random.split(key, 6)
        s = 0.02
        return {'x': jax.random.normal(ks[0], (B, T, C), jnp.float32), 'rw1': s * jax.random.normal(ks[1], (C, H), jnp.float32), 'rb1': jnp.zeros((H,), jnp.float32), 'rw2': s * jax.random.normal(ks[2], (H, E), jnp.float32), 'rb2': jnp.zeros((E,), jnp.float32), 'ew1': s * jax.random.normal(ks[3], (E, C, H), jnp.float32), 'eb1': jnp.zeros((E, H), jnp.float32), 'ew2': s * jax.random.normal(ks[4], (E, H, C), jnp.float32), 'eb2': jnp.zeros((E, C), jnp.float32)}
    _L0_ffn_all = _L0_ffn_setup()
    _L0_ffn_in = {k: v for k, v in _L0_ffn_all.items() if k in ('rw1', 'rb1', 'rw2', 'rb2', 'ew1', 'eb1', 'ew2', 'eb2')}
    del _L0_ffn_all
    return {'x': x, 'ctx_1024': ctx_1024, 'g_xattn': g_xattn, 'g_ffn': g_ffn, 'L0_xattn_igate_w': _L0_xattn_in['igate_w'], 'L0_xattn_igate_b': _L0_xattn_in['igate_b'], 'L0_xattn_fgate_w': _L0_xattn_in['fgate_w'], 'L0_xattn_fgate_b': _L0_xattn_in['fgate_b'], 'L0_xattn_norm_w': _L0_xattn_in['norm_w'], 'L0_ffn_rw1': _L0_ffn_in['rw1'], 'L0_ffn_rb1': _L0_ffn_in['rb1'], 'L0_ffn_rw2': _L0_ffn_in['rw2'], 'L0_ffn_rb2': _L0_ffn_in['rb2'], 'L0_ffn_ew1': _L0_ffn_in['ew1'], 'L0_ffn_eb1': _L0_ffn_in['eb1'], 'L0_ffn_ew2': _L0_ffn_in['ew2'], 'L0_ffn_eb2': _L0_ffn_in['eb2']}

def reference(x, ctx_1024, g_xattn, g_ffn, L0_xattn_igate_w, L0_xattn_igate_b, L0_xattn_fgate_w, L0_xattn_fgate_b, L0_xattn_norm_w, L0_ffn_rw1, L0_ffn_rb1, L0_ffn_rw2, L0_ffn_rb2, L0_ffn_ew1, L0_ffn_eb1, L0_ffn_ew2, L0_ffn_eb2):
    import jax
    import jax.numpy as jnp

    def _L0_xattn_ref(q, k, v, igate_w, igate_b, fgate_w, fgate_b, norm_w):
        import jax, jax.numpy as jnp
        import numpy as np
        B, S, E, NH = (1, 512, 256, 8)
        DH = E // NH
        EPS_BACKEND = 1e-06
        EPS_NORM = 1e-05
        Bq, Sq, Eq = q.shape
        nh = igate_w.shape[0]
        dh = Eq // nh
        gate_in = jnp.concatenate([q, k, v], axis=-1)
        ig = jnp.transpose(gate_in @ igate_w.T + igate_b, (0, 2, 1))
        fg = jnp.transpose(gate_in @ fgate_w.T + fgate_b, (0, 2, 1))
        qh = q.reshape(Bq, Sq, nh, dh).transpose(0, 2, 1, 3)
        kh = k.reshape(Bq, Sq, nh, dh).transpose(0, 2, 1, 3)
        vh = v.reshape(Bq, Sq, nh, dh).transpose(0, 2, 1, 3)
        log_f_cum = jnp.cumsum(jax.nn.log_sigmoid(fg), axis=-1)
        log_fg_mat = log_f_cum[:, :, :, None] - log_f_cum[:, :, None, :]
        ltr = jnp.tril(jnp.ones((Sq, Sq), dtype=bool))
        log_D = jnp.where(ltr, log_fg_mat + ig[:, :, None, :], -jnp.inf)
        max_log_D = jnp.max(log_D, axis=-1, keepdims=True)
        D = jnp.exp(log_D - max_log_D)
        qk = jnp.einsum('bhsd,bhtd->bhst', qh, kh) / jnp.sqrt(jnp.float32(dh))
        C = qk * D
        normalizer = jnp.maximum(jnp.abs(jnp.sum(C, axis=-1, keepdims=True)), jnp.exp(-max_log_D))
        h = jnp.einsum('bhst,bhtd->bhsd', C / (normalizer + EPS_BACKEND), vh)
        mean = jnp.mean(h, axis=-1, keepdims=True)
        var = jnp.var(h, axis=-1, keepdims=True)
        h_norm = (h - mean) / jnp.sqrt(var + EPS_NORM)
        h_norm = h_norm * norm_w.reshape(nh, dh)[None, :, None, :]
        return h_norm.transpose(0, 2, 1, 3).reshape(Bq, Sq, Eq)

    def _L0_ffn_ref(x, rw1, rb1, rw2, rb2, ew1, eb1, ew2, eb2):
        import jax, jax.numpy as jnp
        import numpy as np
        B, T, C, E, K, CAP, H = (8, 512, 256, 8, 2, 1024, 1024)
        Bx, Tx, Cx = x.shape
        N = Bx * Tx
        logits = jax.nn.relu(x @ rw1 + rb1) @ rw2 + rb2
        vals, ids = jax.lax.top_k(logits, K)
        probs = jax.nn.softmax(vals, axis=-1)
        ids_f = ids.reshape(N * K)
        probs_f = probs.reshape(N * K)
        xr = jnp.repeat(x.reshape(N, Cx), K, axis=0)
        m = jax.nn.one_hot(ids_f, E, dtype=jnp.int32)
        pos = jnp.cumsum(m, axis=0) - 1
        pos_tok = jnp.take_along_axis(pos, ids_f[:, None], axis=1)[:, 0]
        keep = (pos_tok < CAP).astype(x.dtype)
        pos_c = jnp.clip(pos_tok, 0, CAP - 1)
        disp = jnp.zeros((E, CAP, Cx), x.dtype).at[ids_f, pos_c].add(xr * keep[:, None])
        h = jax.nn.relu(jnp.einsum('enc,ech->enh', disp, ew1) + eb1[:, None, :])
        eo = jnp.einsum('enh,ehc->enc', h, ew2) + eb2[:, None, :]
        y = eo[ids_f, pos_c] * (probs_f * keep)[:, None]
        return y.reshape(Bx, Tx, K, Cx).sum(axis=2)
    x = x + jnp.tanh(g_xattn[0]) * _L0_xattn_ref(_layernorm(x, axis=-1), ctx_1024, ctx_1024, L0_xattn_igate_w, L0_xattn_igate_b, L0_xattn_fgate_w, L0_xattn_fgate_b, L0_xattn_norm_w)
    x = x + jnp.tanh(g_ffn[0]) * _L0_ffn_ref(_layernorm(x, axis=-1), L0_ffn_rw1, L0_ffn_rb1, L0_ffn_rw2, L0_ffn_rb2, L0_ffn_ew1, L0_ffn_eb1, L0_ffn_ew2, L0_ffn_eb2)
    return x

_drawn_inputs = setup_inputs


def setup_inputs(seed=0):
    import zlib

    import numpy as np

    out = dict(_drawn_inputs(seed))
    spreads = {'L0_ffn_rb1': (0.0, 0.1),
     'L0_ffn_rb2': (0.0, 0.1),
     'L0_ffn_eb1': (0.0, 0.452),
     'L0_ffn_eb2': (0.0, 0.1)}
    factors = {'L0_xattn_igate_b': 64.0, 'L0_xattn_fgate_w': 2.794}
    for name, (base, spread) in spreads.items():
        noise = np.random.default_rng([zlib.crc32(name.encode()), seed]).standard_normal(out[name].shape)
        drawn = base * np.exp(spread * noise) if base else spread * noise
        out[name] = jnp.asarray(drawn.astype(out[name].dtype))
    for name, factor in factors.items():
        out[name] = (out[name] * factor).astype(out[name].dtype)
    return out
```

```python
from contextlib import ExitStack

import numpy as np
import concourse.bass as bass
from concourse import mybir

ALU = mybir.AluOpType
ACT = mybir.ActivationFunctionType
AXX = mybir.AxisListType.X
F32 = mybir.dt.float32
BF16 = mybir.dt.bfloat16
I32 = mybir.dt.int32
U32 = mybir.dt.uint32

P = 128
NB, S, C = 16, 128, 256
NH, DH = 8, 32
N = NB * S
H = 1024
NE, TOPK, CAP = 8, 2, 1024
KC = C // P
KH = H // P
TILES = (N * TOPK + NE * (P - 1)) // P
SLOTS = NE * CAP
EMPTY_ROW = SLOTS
UB = 3
assert TILES % UB == 0 and NB % 2 == 0
EPS_LN, EPS_DEN = 1e-5, 1e-6
SCALE = float(DH) ** -0.5
NEG = -1.0e30


class Count:

    def __init__(self, sem):
        self.sem, self.n = sem, 0

    def inc(self, ins):
        ins.then_inc(self.sem, 1)
        self.n += 1

    def wait(self, eng):
        if self.n:
            eng.wait_ge(self.sem, self.n)

    def restart(self, eng):
        self.wait(eng)
        eng.sem_clear(self.sem)
        self.n = 0


def reached(eng, sem, value):
    if isinstance(value, int) and value <= 0:
        return
    eng.wait_ge(sem, value)


def flags(j):
    return dict(front=j < NB // 2, d0=1 <= j <= NB // 2, d1=j < NB // 2,
                ra=1 <= j <= NB // 2, rb=2 <= j <= NB // 2 + 1)


BODIES = NB // 2 + 2
FULL = (3, NB // 2)


def build(nc, x, ctx_in, g_x, g_f, wg, gb, norm_w, rw1, rb1t, rw2, rb2, ew1, eb1t, ew2, eb2,
          cst, tri_in, tokids, meta_init, out):
    def dram(name, shape, dt):
        return nc.dram_tensor(name, shape, dt, kind="Internal").ap()

    m_dram = dram("m_dram", (NB, NH * S), F32)
    xf_tab = dram("xf_tab", (N + P, C), F32)
    meta_tab = dram("meta_tab", (SLOTS + P, 2), I32)

    with ExitStack() as stack:
        def sb(name, shape, dt=F32):
            return stack.enter_context(nc.sbuf_tensor(name, shape, dt))

        def sem(name):
            return stack.enter_context(nc.semaphore(name))

        ps = stack.enter_context(nc.psum_tensor("ps", [P, 8, 512], F32))

        ident = sb("ident", [P, P])
        triu_incl = sb("triu_incl", [P, P])
        iota_e = sb("iota_e", [P, NE])
        blk_thr = sb("blk_thr", [1, 8])
        tile_id = sb("tile_id", [1, TILES])
        exp_row = sb("exp_row", [1, NE])
        tri = sb("tri", [P, 2, P], BF16)
        tok_sb = sb("tok_sb", [P, NB], I32)
        w_gate = sb("w_gate", [P, 6, 16])
        w_gc = sb("w_gc", [P, 4, 16])
        gate_b = sb("gate_b", [P, 16])
        norm_sb = sb("norm_sb", [P, C])
        normg = sb("normg", [P, C])
        g2 = sb("g2", [P, 2])
        tg = sb("tg", [P, 2])
        rw1_sb = sb("rw1_sb", [P, KC, H])
        rb1_sb = sb("rb1_sb", [P, KH])
        rw2_sb = sb("rw2_sb", [P, KH, NE])
        rb2_sb = sb("rb2_sb", [P, NE])
        w1 = sb("w1", [P, NE, KC, H])
        w2 = sb("w2", [P, NE, KH, C])
        b1 = sb("b1", [P, NE, KH])
        b2 = sb("b2", [P, NE, C])
        zeros = sb("zeros", [P, C])

        x_all = sb("x_all", [P, 4, C])
        ctx_sb = sb("ctx_sb", [P, 2, C])
        stats = sb("stats", [P, 6])
        mv = sb("mv", [P, 2])
        spare = sb("spare", [P, 1])
        vare = sb("vare", [P, 1])
        rstd = sb("rstd", [P, 1])
        half = sb("half", [P, 8])
        rs = sb("rs", [P, 8])
        xn = sb("xn", [P, C])
        qkT = sb("qkT", [P, 2, 4, P])
        v33 = sb("v33", [P, 2, NH, DH + 1])
        gts = sb("gts", [P, 16])
        nab = sb("nab", [P, 8])
        ex = sb("ex", [P, 8])
        lp = sb("lp", [P, 8])
        lf = sb("lf", [P, 8])
        fcum = sb("fcum", [P, 8])
        a_sb = sb("a_sb", [P, 2, 8])
        m_sb = sb("m_sb", [P, P])
        fm = sb("fm", [P, 8])
        nm = sb("nm", [P, 2, 8])
        m_bc = sb("m_bc", [P, 2, NH * S])
        d_sb = sb("d_sb", [P, NH * S])
        c_sb = sb("c_sb", [P, NH * S])
        nrm = sb("nrm", [P, 8])
        rowsum = sb("rowsum", [P, 8])
        den = sb("den", [P, 8])
        hv = sb("hv", [P, 8, DH])
        sm = sb("sm", [P, 8])
        hc = sb("hc", [P, 8, DH])
        sq = sb("sq", [P, 8, DH])
        vs = sb("vs", [P, 8])
        hn = sb("hn", [P, 8, DH])
        xr = sb("xr", [P, 2, C])
        xf = sb("xf", [P, 2, C])
        xfT = sb("xfT", [P, KC, 2 * P])
        hbuf = sb("hbuf", [P, KH, 2 * P])
        lg = sb("lg", [P, 2, NE])
        mx = sb("mx", [P, 2, 8])
        mi = sb("mi", [P, 2, 8], U32)
        mif = sb("mif", [P, 2, 2])
        dd = sb("dd", [P, 2, 1])
        ee = sb("ee", [P, 2, 1])
        s1 = sb("s1", [P, 2, 1])
        pr = sb("pr", [P, 2, 2])
        oh = sb("oh", [P, 2, 2, NE])
        mask = sb("mask", [P, 2, NE], BF16)
        before = sb("before", [P, 2, NE], BF16)
        pm = sb("pm", [P, 2, 2, NE])
        pos = sb("pos", [P, 2, 2])
        over = sb("over", [P, 2, 2])
        slot = sb("slot", [P, 2, 2])
        slot_i = sb("slot_i", [P, 4], I32)
        meta = sb("meta", [P, 4, 2], I32)

        cnt = sb("cnt", [1, NE])
        blk = sb("blk", [1, NE, 8])
        nblk = sb("nblk", [1, NE])
        ones_r = sb("ones_r", [1, NE])
        end = sb("end", [1, NE])
        start = sb("start", [1, NE])
        base = sb("base", [1, NE])
        ge, gs, inr, rowc = (m_bc[0:1, k, q * 512:q * 512 + TILES * NE].rearrange("p (t e) -> p t e", e=NE)
                             for k, q in ((0, 0), (0, 1), (1, 0), (1, 1)))
        eidx = sb("eidx", [1, TILES])
        rsum = sb("rsum", [1, TILES])
        emp = sb("emp", [1, TILES])
        sched_row = sb("sched_row", [1, TILES], I32)
        sched_e = sb("sched_e", [1, TILES], I32)

        meta_g = sb("meta_g", [P, UB, 2], I32)
        meta_s = sb("meta_s", [P, UB, 2], I32)
        xg = d_sb[:, 0:UB * C].rearrange("p (u c) -> p u c", u=UB)
        xT = sb("xT", [P, KC, P])
        h_sb = hbuf[:, 0:4, :].rearrange("p m t -> p (m t)")
        hT = hbuf[:, 4:8, :].rearrange("p m t -> p (m t)").rearrange("p (m t) -> p m t", m=KH)
        hpre = c_sb[:, :].rearrange("p (m t) -> p m t", m=KH)
        yb = sb("yb", [P, C])
        y = qkT[:].rearrange("p u c t -> p (u c t)")[:, 0:UB * C].rearrange("p (u c) -> p u c", u=UB)

        S4 = ps[:, 0:4, 0:256]
        O2 = ps[:, 0:2, 256:256 + 4 * (DH + 1)]
        O4 = O2.rearrange("p g (j d) -> p g j d", j=4)
        PFX = ps[:, 2, 256:256 + 2 * NE].rearrange("p (b e) -> p b e", b=2)
        CNT = ps[:, 2, 256:256 + NE]
        LG = ps[:, 3, 256:256 + 2 * NE].rearrange("p (b e) -> p b e", b=2)
        T4 = ps[:, 4, :].rearrange("p (c t) -> p c t", c=4)
        GT = ps[:, 5, 0:16]
        FC = ps[:, 5, 16:24]
        AT = ps[0:8, 5, 24:24 + P]
        MT = ps[:, 5, 160:160 + P]

        def RH(m):
            return ps[:, 6 + m % 2, 0:2 * P]

        HP = ps[:, 0:2, :]
        HT = ps[:, 2:4, :].rearrange("p b (m t) -> p (b m) t", m=4)
        YP = ps[:, 4, 0:C]
        XT = ps[:, 5, 0:KC * P].rearrange("p (c t) -> p c t", c=KC)

        cst_in = sem("cst_in")
        tri_loaded = sem("tri_loaded")
        tables_init = sem("tables_init")
        weights_in = sem("weights_in")
        x_in = [sem(f"x_in{u}") for u in range(2)]
        ctx_in_s = [sem(f"ctx_in{u}") for u in range(2)]
        setup_dve = sem("setup_dve")
        setup_pool = sem("setup_pool")
        tanh_ready = sem("tanh_ready")
        xn_ready = sem("xn_ready")
        t_done = sem("t_done")
        qkT_ready = sem("qkT_ready")
        v33_ready = sem("v33_ready")
        gates_done = sem("gates_done")
        nab_ready = sem("nab_ready")
        ex_ready = sem("ex_ready")
        lp_ready = sem("lp_ready")
        lf_ready = sem("lf_ready")
        f_done = sem("f_done")
        a_ready = sem("a_ready")
        at_done = sem("at_done")
        m_ready = sem("m_ready")
        m_stored = sem("m_stored")
        m_bc_in = [sem(f"m_bc_in{u}") for u in range(2)]
        mt_done = sem("mt_done")
        fm_ready = sem("fm_ready")
        nm_ready = sem("nm_ready")
        s_done = sem("s_done")
        arg_ready = sem("arg_ready")
        masked = sem("masked")
        d_ready = sem("d_ready")
        c_ready = sem("c_ready")
        pv_done = sem("pv_done")
        o_read = sem("o_read")
        hn_ready = sem("hn_ready")
        pool_step = sem("pool_step")
        xr_ready = sem("xr_ready")
        xf_ready = sem("xf_ready")
        rows_out = [sem(f"rows_out{u}") for u in range(2)]
        xf_t_done = sem("xf_t_done")
        xfT_ready = sem("xfT_ready")
        rh_done = sem("rh_done")
        rh_ready = sem("rh_ready")
        lg_done = sem("lg_done")
        diff_ready = sem("diff_ready")
        ee_ready = sem("ee_ready")
        mask_ready = sem("mask_ready")
        pfx_done = sem("pfx_done")
        pfx_read = sem("pfx_read")
        slots_ready = sem("slots_ready")
        slots_sent = sem("slots_sent")
        cnt_done = sem("cnt_done")
        sched_ready = sem("sched_ready")
        var_x, rstd_x = sem("var_x"), sem("rstd_x")
        var_h, rstd_h = sem("var_h"), sem("rstd_h")
        var_r, rstd_r = sem("var_r"), sem("rstd_r")
        dve_step = sem("dve_step")
        act_step = sem("act_step")

        metag_in = [sem(f"metag_in{u}") for u in range(UB)]
        metas_in = [sem(f"metas_in{u}") for u in range(UB)]
        gathered = [sem(f"gathered{u}") for u in range(UB)]
        scattered = [sem(f"scattered{u}") for u in range(UB)]
        xt_done = sem("xt_done")
        xT_ready = sem("xT_ready")
        l1_done = sem("l1_done")
        h_act = sem("h_act")
        h_dve = sem("h_dve")
        ht_done = sem("ht_done")
        hpre_ready = sem("hpre_ready")
        hT_ready = sem("hT_ready")
        l2_done = sem("l2_done")
        yb_ready = sem("yb_ready")
        y_ready = sem("y_ready")

        N_CST = 17
        block = stack.enter_context(nc.Block())

        def consts(eng):
            eng.wait_ge(cst_in, 16 * N_CST)

        def pool_waits(pool, step, *conditions):
            step.wait(pool)
            for sm_, v in conditions:
                reached(pool, sm_, v)
            step.inc(pool.tensor_tensor(spare[:], half[:, 0:1], half[:, 0:1], ALU.add))
            pool.wait_ge(setup_pool, 4)
            for sm_, v in conditions:
                reached(pool, sm_, v)

        @block.sync
        def _(sp):
            def load_batch(i, u):
                sp.dma_start(x_all[:, bass.ds(i % 4, 1), :].rearrange("p a c -> p (a c)"),
                             x[bass.ds(i, 1), :, :].rearrange("a p c -> (a p) c")).then_inc(x_in[u], 16)
                sp.dma_start(ctx_sb[:, u, :],
                             ctx_in[bass.ds(i, 1), :, :].rearrange("a p c -> (a p) c")).then_inc(ctx_in_s[u], 16)

            load_batch(0, 0)
            for dst, src in ((ident, cst[:, 0:P]), (triu_incl, cst[:, P:2 * P]),
                             (iota_e, cst[:, 2 * P:2 * P + NE]),
                             (blk_thr, cst[0:1, 264:272]), (exp_row, cst[0:1, 272:280]),
                             (tile_id, cst[0:1, 280:280 + TILES]), (tok_sb, tokids),
                             (w_gate, wg), (gate_b, gb.partition_broadcast(P)),
                             (norm_sb, norm_w.partition_broadcast(P)),
                             (rb1_sb, rb1t), (rw2_sb, rw2.rearrange("(m p) e -> p m e", p=P)),
                             (rb2_sb, rb2.partition_broadcast(P)), (b1, eb1t)):
                d = dst[:]
                sp.dma_start(d, src).then_inc(cst_in, 16)
            sp.dma_start(g2[:, 0:1], g_x.partition_broadcast(P)).then_inc(cst_in, 16)
            sp.dma_start(g2[:, 1:2], g_f.partition_broadcast(P)).then_inc(cst_in, 16)
            sp.dma_start(b2[:].rearrange("p e c -> p (e c)"),
                         eb2.rearrange("e c -> (e c)").partition_broadcast(P)).then_inc(cst_in, 16)
            sp.dma_start(tri[:], tri_in).then_inc(tri_loaded, 16)
            load_batch(1, 1)
            sp.dma_start(rw1_sb[:], rw1.rearrange("(k p) h -> p k h", p=P)).then_inc(tri_loaded, 16)
            sp.dma_start(meta_tab, meta_init).then_inc(tables_init, 16)
            sp.wait_ge(setup_pool, 2)
            sp.dma_start(xf_tab[N:N + P, :], zeros[:]).then_inc(tables_init, 16)
            sp.dma_start(out[N:N + P, :], zeros[:]).then_inc(tables_init, 16)

            def body(j, f):
                for u in range(2):
                    i = 2 * j + u
                    if f["front"]:
                        sp.wait_ge(m_ready, i + 1)
                        sp.dma_start(m_dram[bass.ds(i, 1), :].rearrange("a (h s) -> (a h) s", h=NH),
                                     m_sb[0:8, :]).then_inc(m_stored, 16)
                        sp.wait_ge(m_stored, 16 * (i + 1))
                        sp.dma_start(m_bc[:, u, :],
                                     m_dram[bass.ds(i, 1), :].rearrange("a n -> (a n)").partition_broadcast(P)
                                     ).then_inc(m_bc_in[u], 16)
                    if f["front"] and f["more"]:
                        reached(sp, xr_ready, i - 1)
                        sp.wait_ge(t_done, i + 1)
                        sp.wait_ge(v33_ready, i + 1)
                        load_batch(i + 2, u)
                    if f["d0"] if u == 0 else f["d1"]:
                        b = i - 1
                        sp.wait_ge(xf_ready, b + 1)
                        sp.dma_start(out[bass.ds(b * P, P), :], xr[:, 1 - u, :]).then_inc(rows_out[1 - u], 16)
                        sp.dma_start(xf_tab[bass.ds(b * P, P), :], xf[:, 1 - u, :]).then_inc(rows_out[1 - u], 16)
                    if u == 1 and f["front"]:
                        sp.dma_start(w1[:, bass.ds(j, 1), :, :].rearrange("p a k h -> p (a k) h"),
                                     ew1[bass.ds(j, 1), :, :].rearrange("a (k p) h -> p (a k) h", p=P)
                                     ).then_inc(weights_in, 16)
                        sp.dma_start(w2[:, bass.ds(j, 1), :, :].rearrange("p a m c -> p (a m) c"),
                                     ew2[bass.ds(j, 1), :, :].rearrange("a (m p) c -> p (a m) c", p=P)
                                     ).then_inc(weights_in, 16)

            run_bodies(sp, body)

            sp.wait_ge(sched_ready, 1)
            sp.wait_ge(slots_sent, 16 * 4 * (NB // 2))

            def load_meta(row, u, dst, s):
                sp.dma_start(dst[:, u, :], meta_tab[bass.ds(row, P), :]).then_inc(s, 16)

            def tile_body(j, first):
                for u in range(UB):
                    row = sp.value_load(sched_row[0:1, bass.ds(UB * j + u, 1)], min_val=0, max_val=SLOTS)
                    if not first:
                        sp.wait_ge(gathered[u], 16 * j)
                    load_meta(row, u, meta_g, metag_in[u])
                    if not first:
                        sp.wait_ge(scattered[u], 16 * j)
                    load_meta(row, u, meta_s, metas_in[u])

            tile_body(0, True)
            with sp.Fori(1, TILES // UB) as j:
                tile_body(j, False)
            for u in range(UB):
                sp.wait_ge(scattered[u], 16 * (TILES // UB))
                sp.wait_ge(metas_in[u], 16 * (TILES // UB))
            for u in range(2):
                sp.wait_ge(rows_out[u], 32 * (NB // 2))

        @block.tensor
        def _(pe):
            def transposes_T(i, u, pairs_before):
                pe.wait_ge(xn_ready, i + 1)
                pe.wait_ge(ctx_in_s[u], pairs_before[0])
                reached(pe, qkT_ready, i)
                reached(pe, xfT_ready, pairs_before[1])
                for c in range(2):
                    pe.transpose(T4[:, c, :], xn[:, c * P:(c + 1) * P], ident[:])
                for c in range(2):
                    ins = pe.transpose(T4[:, 2 + c, :], ctx_sb[:, u, c * P:(c + 1) * P], ident[:])
                ins.then_inc(t_done, 1)

            def gates(i, u):
                pe.wait_ge(qkT_ready, i + 1)
                reached(pe, fm_ready, i)
                for c in range(4):
                    ins = pe.matmul(GT, qkT[:, u, c, :], w_gc[:, c, :], start=(c == 0), stop=(c == 3))
                ins.then_inc(gates_done, 1)

            def fcumsum(i):
                pe.wait_ge(lf_ready, i + 1)
                pe.matmul(FC, triu_incl[:], lf[:], start=True, stop=True).then_inc(f_done, 1)

            def a_transpose(i, u):
                pe.wait_ge(a_ready, i + 1)
                pe.transpose(AT, a_sb[:, u, :], ident[:]).then_inc(at_done, 1)

            def m_transpose(i):
                pe.wait_ge(m_ready, i + 1)
                pe.transpose(MT, m_sb[:], ident[:]).then_inc(mt_done, 1)

            def scores(b, u):
                pe.wait_ge(qkT_ready, b + 1)
                reached(pe, o_read, b)
                for g in range(2):
                    for r in range(4):
                        rows = slice(DH * r, DH * (r + 1))
                        ins = pe.matmul(S4[:, r, g * P:(g + 1) * P], qkT[rows, u, 2 + g, :], qkT[rows, u, g, :],
                                        start=True, stop=True, tile_position=(DH * r, 0))
                ins.then_inc(s_done, 1)

            def pv(b, u):
                pe.wait_ge(c_ready, b + 1)
                pe.wait_ge(v33_ready, b + 1)
                for h in range(NH):
                    hh = (h % 4) * 2 + h // 4
                    ins = pe.matmul(O4[:, h // 4, h % 4, :], c_sb[:, hh * P:(hh + 1) * P], v33[:, u, h, :],
                                    start=True, stop=True)
                ins.then_inc(pv_done, 1)

            def router_T(p):
                pe.wait_ge(xf_ready, 2 * p + 2)
                pe.wait_ge(qkT_ready, 2 * p + 4 if not isinstance(p, int) else min(2 * p + 4, NB))
                for b in range(2):
                    for c in range(2):
                        ins = pe.transpose(T4[:, 2 * c + b, :], xf[:, b, c * P:(c + 1) * P], ident[:])
                ins.then_inc(xf_t_done, 1)

            def router_hidden(p, m):
                pe.wait_ge(xfT_ready, p + 1)
                reached(pe, rh_ready, KH * p + m - 1)
                for k in range(KC):
                    ins = pe.matmul(RH(m), rw1_sb[:, k, m * P:(m + 1) * P], xfT[:, k, :],
                                    start=(k == 0), stop=(k == KC - 1))
                ins.then_inc(rh_done, 1)

            def router_logits(p):
                pe.wait_ge(rh_ready, KH * (p + 1))
                for b in range(2):
                    for m in range(KH):
                        ins = pe.matmul(LG[:, b, :], hbuf[:, m, b * P:(b + 1) * P], rw2_sb[:, m, :],
                                        start=(m == 0), stop=(m == KH - 1))
                ins.then_inc(lg_done, 1)

            def prefix(p):
                pe.wait_ge(mask_ready, p + 1)
                for b in range(2):
                    pe.matmul(PFX[:, b, :], tri[:, 0, :], mask[:, b, :], start=True, stop=False)
                    ins = pe.matmul(PFX[:, b, :], tri[:, 1, :], before[:, b, :], start=False, stop=True)
                ins.then_inc(pfx_done, 1)

            def body(j, f):
                i = 2 * j
                front, d0, d1, ra, rb = f["front"], f["d0"], f["d1"], f["ra"], f["rb"]
                if d0:
                    if rb:
                        pe.wait_ge(pfx_read, j - 2)
                    scores(i - 1, 1)
                if front:
                    transposes_T(i, 0, (16 * (j + 1), j - 1))
                if rb:
                    router_hidden(j - 2, 4)
                    router_hidden(j - 2, 5)
                if front:
                    gates(i, 0)
                if rb:
                    router_hidden(j - 2, 6)
                if d0:
                    pv(i - 1, 1)
                if front:
                    fcumsum(i)
                if rb:
                    router_hidden(j - 2, 7)
                if front:
                    a_transpose(i, 0)
                if rb:
                    router_logits(j - 2)
                if front:
                    m_transpose(i)
                if d1:
                    if rb:
                        pe.wait_ge(mask_ready, j - 1)
                    scores(i, 0)
                if front:
                    transposes_T(i + 1, 1, (16 * (j + 1), j - 1))
                if ra:
                    router_T(j - 1)
                if front:
                    gates(i + 1, 1)
                if d1:
                    pv(i, 0)
                if rb:
                    prefix(j - 2)
                if front:
                    fcumsum(i + 1)
                if ra:
                    router_hidden(j - 1, 0)
                if front:
                    a_transpose(i + 1, 1)
                if ra:
                    router_hidden(j - 1, 1)
                    router_hidden(j - 1, 2)
                if front:
                    m_transpose(i + 1)
                if ra:
                    router_hidden(j - 1, 3)

            consts(pe)
            pe.wait_ge(tri_loaded, 32)
            pe.wait_ge(setup_dve, 1)
            run_bodies(pe, body)

            pe.wait_ge(pfx_read, NB // 2)
            pe.matmul(CNT, tri[:, 1, :], before[:, 0, :], start=True, stop=True).then_inc(cnt_done, 1)

            pe.wait_ge(sched_ready, 1)
            pe.wait_ge(weights_in, 32 * NE)

            def expert(i):
                return pe.value_load(sched_e[0:1, bass.ds(i, 1)], min_val=0, max_val=NE - 1)

            def x_transpose(i, u, j):
                pe.wait_ge(gathered[u], 16 * (j + 1))
                reached(pe, xT_ready, i)
                for c in range(KC):
                    ins = pe.transpose(XT[:, c, :], xg[:, u, c * P:(c + 1) * P], ident[:])
                ins.then_inc(xt_done, 1)

            def layer1(i, e):
                pe.wait_ge(xT_ready, i + 1)
                reached(pe, h_act, i)
                reached(pe, h_dve, i)
                for n in range(2):
                    for k in range(KC):
                        ins = pe.matmul(HP[:, n, :], xT[:, k, :],
                                        w1[:, bass.ds(e, 1), k, n * 512:(n + 1) * 512].rearrange("p a n -> p (a n)"),
                                        start=(k == 0), stop=(k == KC - 1))
                ins.then_inc(l1_done, 1)

            def h_transpose(i):
                pe.wait_ge(h_act, i + 1)
                pe.wait_ge(h_dve, i + 1)
                reached(pe, hpre_ready, i)
                for m in range(KH):
                    ins = pe.transpose(HT[:, m, :], h_sb[:, m * P:(m + 1) * P], ident[:])
                ins.then_inc(ht_done, 1)

            def layer2(i, e):
                pe.wait_ge(hT_ready, i + 1)
                reached(pe, yb_ready, i)
                for m in range(KH):
                    ins = pe.matmul(YP, hT[:, m, :],
                                    w2[:, bass.ds(e, 1), m, :].rearrange("p a n -> p (a n)"),
                                    start=(m == 0), stop=(m == KH - 1))
                ins.then_inc(l2_done, 1)

            def tile_body(j, first, last):
                for u in range(UB):
                    i = UB * j + u
                    e = expert(i)
                    layer1(i, e)
                    if not (first and u == 0):
                        layer2(i - 1, expert(i - 1))
                    if not (last and u == UB - 1):
                        x_transpose(i + 1, (u + 1) % UB, j + (u + 1) // UB)
                    h_transpose(i)

            x_transpose(0, 0, 0)
            tile_body(0, True, False)
            with pe.Fori(1, TILES // UB - 1) as j:
                tile_body(j, False, False)
            tile_body(TILES // UB - 1, False, True)
            layer2(TILES - 1, expert(TILES - 1))

        @block.vector
        def _(ve):
            chain = Count(dve_step)

            def link(ins):
                chain.inc(ins)
                chain.wait(ve)

            def layernorm(src, dst, done, var_sem, rstd_sem, value):
                link(ve.bn_stats(stats[:], src))
                link(ve.bn_aggr(mv[:], stats[:]))
                ve.tensor_scalar(vare[:], mv[:, 1:2], EPS_LN, None, ALU.add).then_inc(var_sem, 1)
                ve.wait_ge(rstd_sem, value)
                ve.tensor_scalar(dst, src, mv[:, 0:1], rstd[:, 0:1], ALU.subtract, ALU.mult).then_inc(done, 1)

            def norm_x(i, u, loads):
                ve.wait_ge(x_in[u], loads)
                reached(ve, t_done, i)
                layernorm(x_all[:, bass.ds(i % 4, 1), :].rearrange("p a c -> p (a c)"), xn[:], xn_ready, var_x, rstd_x, i + 1)

            def gate1(i):
                ve.wait_ge(gates_done, i + 1)
                link(ve.tensor_tensor(gts[:], GT, gate_b[:], ALU.add))
                reached(ve, ex_ready, i)
                ve.scalar_tensor_tensor(nab[:], gts[:, 8:16], -1.0, gts[:, 8:16], ALU.mult, ALU.min).then_inc(nab_ready, 1)

            def logsig(i):
                ve.wait_ge(lp_ready, i + 1)
                reached(ve, f_done, i)
                ve.scalar_tensor_tensor(lf[:], gts[:, 8:16], 0.0, lp[:], ALU.min, ALU.subtract).then_inc(lf_ready, 1)

            def a_vals(i, u):
                ve.wait_ge(f_done, i + 1)
                link(ve.tensor_copy(fcum[:], FC))
                ve.tensor_tensor(a_sb[:, u, :], gts[:, 0:8], fcum[:], ALU.subtract).then_inc(a_ready, 1)

            def running_max(i):
                ve.wait_ge(at_done, i + 1)
                reached(ve, m_stored, 16 * i)
                reached(ve, mt_done, i)
                ve.tensor_tensor_scan(m_sb[0:8, :], zeros[0:8, 0:P], AT, -3.0e38, ALU.add, ALU.max).then_inc(m_ready, 1)

            def f_plus_m(i):
                ve.wait_ge(mt_done, i + 1)
                reached(ve, nm_ready, i)
                ve.tensor_tensor(fm[:], fcum[:], MT[:, 0:8], ALU.add).then_inc(fm_ready, 1)

            def decay_arg(b, u, loads):
                ve.wait_ge(m_bc_in[u], loads)
                reached(ve, c_ready, b)
                ve.wait_ge(a_ready, b + 1)
                ve.tensor_tensor(d_sb[:].rearrange("p (h s) -> p h s", h=NH),
                                 a_sb[:, u, :].unsqueeze(2).broadcast_to([P, NH, S]),
                                 m_bc[:, u, :].rearrange("p (h s) -> p h s", h=NH),
                                 ALU.subtract).then_inc(arg_ready, 1)

            def weigh(b):
                ve.wait_ge(s_done, b + 1)
                ve.wait_ge(d_ready, b + 1)
                reached(ve, pv_done, b)
                ve.scalar_tensor_tensor(c_sb[:].rearrange("p (r n) -> p r n", r=4), S4, SCALE,
                                        d_sb[:].rearrange("p (r n) -> p r n", r=4),
                                        ALU.mult, ALU.mult).then_inc(c_ready, 1)

            def finish_attention(b, u):
                ve.wait_ge(pv_done, b + 1)
                ve.wait_ge(nm_ready, b + 1)
                nrm2 = nrm[:].rearrange("p (g r) -> p g r", g=2)
                link(ve.tensor_copy(rowsum[:].rearrange("p (g r) -> p g r", g=2), O4[:, :, :, DH]))
                link(ve.scalar_tensor_tensor(nrm[:], rowsum[:], -1.0, rowsum[:], ALU.mult, ALU.max))
                link(ve.tensor_tensor(nrm2, nrm2, nm[:, u, :].rearrange("p (r g) -> p g r", g=2), ALU.max))
                link(ve.tensor_scalar(nrm[:], nrm[:], EPS_DEN, None, ALU.add))
                link(ve.reciprocal(den[:], nrm[:]))
                ve.tensor_tensor(hv[:].rearrange("p (g r) d -> p g r d", g=2), O4[:, :, :, 0:DH],
                                 den[:].rearrange("p (g r) -> p g r", g=2).unsqueeze(3).broadcast_to([P, 2, 4, DH]),
                                 ALU.mult).then_inc(o_read, 1)
                ve.wait_ge(o_read, b + 1)
                link(ve.tensor_reduce(sm[:], hv[:], AXX, ALU.add))
                link(ve.tensor_scalar(sm[:], sm[:], 1.0 / DH, None, ALU.mult))
                link(ve.tensor_tensor(hc[:], hv[:], sm[:].unsqueeze(2).broadcast_to([P, 8, DH]), ALU.subtract))
                link(ve.tensor_tensor(sq[:], hc[:], hc[:], ALU.mult))
                link(ve.tensor_reduce(vs[:], sq[:], AXX, ALU.add))
                ve.tensor_scalar(vs[:], vs[:], 1.0 / DH, EPS_LN, ALU.mult, ALU.add).then_inc(var_h, 1)
                ve.wait_ge(rstd_h, b + 1)
                reached(ve, xr_ready, b)
                ve.tensor_tensor(hn[:], hc[:], rs[:].unsqueeze(2).broadcast_to([P, 8, DH]),
                                 ALU.mult).then_inc(hn_ready, 1)

            def norm_res(b, u, stored, transposed):
                ve.wait_ge(xr_ready, b + 1)
                reached(ve, rows_out[u], stored)
                reached(ve, xf_t_done, transposed)
                layernorm(xr[:, u, :], xf[:, u, :], xf_ready, var_r, rstd_r, b + 1)

            def choose(p):
                ve.wait_ge(lg_done, p + 1)
                link(ve.tensor_tensor(lg[:], LG, rb2_sb[:].unsqueeze(1).broadcast_to([P, 2, NE]), ALU.add))
                for b in range(2):
                    link(ve.max(mx[:, b, :], lg[:, b, :]))
                for b in range(2):
                    link(ve.max_index(mi[:, b, :], mx[:, b, :], lg[:, b, :]))
                reached(ve, ee_ready, p)
                ve.tensor_tensor(dd[:], mx[:, :, 1:2], mx[:, :, 0:1], ALU.subtract).then_inc(diff_ready, 1)
                link(ve.tensor_copy(mif[:], mi[:, :, 0:2]))
                link(ve.tensor_tensor(oh[:], iota_e[:].unsqueeze(1).unsqueeze(1).broadcast_to([P, 2, 2, NE]),
                                      mif[:].unsqueeze(3).broadcast_to([P, 2, 2, NE]), ALU.is_equal))
                link(ve.tensor_tensor(mask[:], oh[:, :, 0, :], oh[:, :, 1, :], ALU.add))
                ve.tensor_tensor(before[:, 1, :], before[:, 0, :], mask[:, 0, :], ALU.add).then_inc(mask_ready, 1)
                ve.wait_ge(ee_ready, p + 1)
                link(ve.tensor_scalar(s1[:], ee[:], 1.0, None, ALU.add))
                link(ve.reciprocal(pr[:, :, 0:1], s1[:]))
                link(ve.tensor_tensor(pr[:, :, 1:2], ee[:], pr[:, :, 0:1], ALU.mult))

            def place(p):
                ve.wait_ge(pfx_done, p + 1)
                link(ve.tensor_tensor(pm[:], oh[:], PFX.unsqueeze(2).broadcast_to([P, 2, 2, NE]), ALU.mult))
                link(ve.tensor_reduce(pos[:], pm[:], AXX, ALU.add))
                link(ve.tensor_scalar(over[:], pos[:], float(CAP), float(4 * SLOTS), ALU.is_ge, ALU.mult))
                link(ve.scalar_tensor_tensor(slot[:], mif[:], float(CAP), pos[:], ALU.mult, ALU.add))
                reached(ve, slots_sent, 64 * p)
                link(ve.tensor_tensor(slot_i[:].rearrange("p (b k) -> p b k", b=2), slot[:], over[:], ALU.add))
                for b in range(2):
                    for k in range(2):
                        link(ve.tensor_copy(meta[:, 2 * b + k, 0:1], tok_sb[:, bass.ds(2 * p + b, 1)]))
                link(ve.tensor_scalar(meta[:].bitcast(F32)[:, :, 1:2].rearrange("p (b k) a -> p b (k a)", b=2),
                                      pr[:], tg[:, 1:2], None, ALU.mult))
                ve.tensor_tensor(before[:, 0, :], before[:, 1, :], mask[:, 1, :], ALU.add).then_inc(slots_ready, 1)
                ve.wait_ge(slots_ready, p + 1)
                ve.tensor_copy(s1[:, 0, :], s1[:, 1, :]).then_inc(pfx_read, 1)

            def body(j, f):
                i = 2 * j
                front, d0, d1, ra, rb = f["front"], f["d0"], f["d1"], f["ra"], f["rb"]
                if d0:
                    decay_arg(i - 1, 1, 16 * j)
                if front:
                    norm_x(i, 0, 16 * (j + 1))
                if front:
                    gate1(i)
                if d0:
                    weigh(i - 1)
                if front:
                    logsig(i)
                    a_vals(i, 0)
                    running_max(i)
                if d0:
                    finish_attention(i - 1, 1)
                if front:
                    f_plus_m(i)
                if d0:
                    norm_res(i - 1, 1, 32 * (j - 1), j - 1)
                if d1:
                    decay_arg(i, 0, 16 * (j + 1))
                if rb:
                    choose(j - 2)
                if front:
                    norm_x(i + 1, 1, 16 * (j + 1))
                    gate1(i + 1)
                if d1:
                    weigh(i)
                if front:
                    logsig(i + 1)
                    a_vals(i + 1, 1)
                if rb:
                    place(j - 2)
                if front:
                    running_max(i + 1)
                if d1:
                    finish_attention(i, 0)
                if front:
                    f_plus_m(i + 1)
                if d1:
                    norm_res(i, 0, 32 * j, j)

            consts(ve)
            ve.wait_ge(tri_loaded, 32)
            ve.wait_ge(setup_pool, 4)
            for c in range(2):
                link(ve.tensor_copy(w_gc[:, c, :], w_gate[:, c, :]))
            ve.wait_ge(tanh_ready, 1)
            link(ve.tensor_scalar(normg[:], norm_sb[:], tg[:, 0:1], None, ALU.mult))
            link(ve.memset(before[:], 0.0))
            ve.tensor_tensor(w_gc[:, 2:4, :], w_gate[:, 2:4, :], w_gate[:, 4:6, :], ALU.add).then_inc(setup_dve, 1)
            run_bodies(ve, body, chain)

            ve.wait_ge(cnt_done, 1)
            link(ve.tensor_copy(cnt[:], CNT[0:1, :]))
            link(ve.tensor_tensor(blk[:], cnt[:].unsqueeze(2).broadcast_to([1, NE, 8]),
                                  blk_thr[:].unsqueeze(1).broadcast_to([1, NE, 8]), ALU.is_gt))
            link(ve.tensor_reduce(nblk[:], blk[:], AXX, ALU.add))
            link(ve.memset(ones_r[:], 1.0))
            link(ve.tensor_tensor_scan(end[:], ones_r[:], nblk[:], 0.0, ALU.mult, ALU.add))
            link(ve.tensor_tensor(start[:], end[:], nblk[:], ALU.subtract))
            link(ve.scalar_tensor_tensor(base[:], start[:], -float(P), exp_row[:], ALU.mult, ALU.add))

            def over_e(a):
                return a.unsqueeze(1).broadcast_to([1, TILES, NE])

            ti = tile_id[:].unsqueeze(2).broadcast_to([1, TILES, NE])
            link(ve.tensor_tensor(ge, ti, over_e(end[:]), ALU.is_ge))
            link(ve.tensor_tensor(gs, ti, over_e(start[:]), ALU.is_ge))
            link(ve.tensor_tensor(inr, gs, ge, ALU.subtract))
            link(ve.tensor_reduce(eidx[:], ge, AXX, ALU.add))
            link(ve.scalar_tensor_tensor(rowc, ti, float(P), over_e(base[:]), ALU.mult, ALU.add))
            link(ve.tensor_tensor(rowc, rowc, inr, ALU.mult))
            link(ve.tensor_reduce(rsum[:], rowc, AXX, ALU.add))
            link(ve.tensor_scalar(emp[:], eidx[:], float(NE), float(EMPTY_ROW), ALU.is_ge, ALU.mult))
            link(ve.tensor_tensor(sched_row[:], rsum[:], emp[:], ALU.add))
            ve.tensor_scalar(sched_e[:], eidx[:], float(NE - 1), None, ALU.min).then_inc(sched_ready, 1)
            ve.wait_ge(sched_ready, 1)

            def expert(i):
                return ve.value_load(sched_e[0:1, bass.ds(i, 1)], min_val=0, max_val=NE - 1)

            def copy_h(i):
                ve.wait_ge(l1_done, i + 1)
                reached(ve, ht_done, i)
                ve.tensor_copy(h_sb[:, 512:1024], HP[:, 1, :]).then_inc(h_dve, 1)

            def bias_h(i, e):
                ve.wait_ge(ht_done, i + 1)
                reached(ve, hT_ready, i)
                ve.tensor_tensor(hpre, HT,
                                 b1[:, bass.ds(e, 1), :].rearrange("p a m -> p (a m)").unsqueeze(2)
                                 .broadcast_to([P, KH, P]), ALU.add).then_inc(hpre_ready, 1)

            def bias_y(i, e):
                ve.wait_ge(l2_done, i + 1)
                reached(ve, y_ready, i)
                ve.tensor_tensor(yb[:], YP, b2[:, bass.ds(e, 1), :].rearrange("p a c -> p (a c)"),
                                 ALU.add).then_inc(yb_ready, 1)

            def tile_body(j, first):
                for u in range(UB):
                    i = UB * j + u
                    copy_h(i)
                    if not (first and u == 0):
                        bias_y(i - 1, expert(i - 1))
                    bias_h(i, expert(i))

            tile_body(0, True)
            with ve.Fori(1, TILES // UB) as j:
                tile_body(j, False)
            bias_y(TILES - 1, expert(TILES - 1))

        @block.scalar
        def _(act):
            def copy_T(i, u):
                act.wait_ge(t_done, i + 1)
                reached(act, s_done, i - 1)
                act.activation(qkT[:, u, :, :].rearrange("p c t -> p (c t)"), ps[:, 4, :], ACT.Copy).then_inc(qkT_ready, 1)

            def log_gate(i):
                act.wait_ge(nab_ready, i + 1)
                act.activation(ex[:], nab[:], ACT.Exp).then_inc(ex_ready, 1)
                act.wait_ge(ex_ready, i + 1)
                reached(act, lf_ready, i)
                act.activation(lp[:], ex[:], ACT.Ln, bias=1.0).then_inc(lp_ready, 1)

            def decay(b):
                act.wait_ge(masked, b + 1)
                act.activation(d_sb[:], d_sb[:], ACT.Exp).then_inc(d_ready, 1)

            def floor_exp(i, u):
                act.wait_ge(fm_ready, i + 1)
                act.activation(nm[:, u, :], fm[:], ACT.Exp, scale=-1.0).then_inc(nm_ready, 1)

            def copy_xfT(p):
                act.wait_ge(xf_t_done, p + 1)
                reached(act, rh_done, KH * p)
                act.activation(xfT[:].rearrange("p k t -> p (k t)"), ps[:, 4, :], ACT.Copy).then_inc(xfT_ready, 1)

            def relu(p, m):
                act.wait_ge(rh_done, KH * p + m + 1)
                reached(act, lg_done, p)
                act.activation(hbuf[:, m, :], RH(m), ACT.Relu, bias=rb1_sb[:, m:m + 1]).then_inc(rh_ready, 1)

            def gate_exp(p):
                act.wait_ge(diff_ready, p + 1)
                act.activation(ee[:], dd[:], ACT.Exp).then_inc(ee_ready, 1)

            def body(j, f):
                i = 2 * j
                front, d0, d1, ra, rb = f["front"], f["d0"], f["d1"], f["ra"], f["rb"]
                if d0:
                    decay(i - 1)
                if front:
                    copy_T(i, 0)
                if rb:
                    relu(j - 2, 4)
                if front:
                    log_gate(i)
                if rb:
                    relu(j - 2, 5)
                    relu(j - 2, 6)
                    relu(j - 2, 7)
                if front:
                    floor_exp(i, 0)
                if d1:
                    decay(i)
                if rb:
                    gate_exp(j - 2)
                if front:
                    copy_T(i + 1, 1)
                if ra:
                    copy_xfT(j - 1)
                if front:
                    log_gate(i + 1)
                if ra:
                    relu(j - 1, 0)
                    relu(j - 1, 1)
                    relu(j - 1, 2)
                if front:
                    floor_exp(i + 1, 1)
                if ra:
                    relu(j - 1, 3)

            consts(act)
            act.activation(tg[:], g2[:], ACT.Tanh).then_inc(tanh_ready, 1)
            run_bodies(act, body)

            def copy_x(i):
                act.wait_ge(xt_done, i + 1)
                reached(act, l1_done, i)
                act.activation(xT[:].rearrange("p k t -> p (k t)"), ps[:, 5, 0:KC * P], ACT.Copy).then_inc(xT_ready, 1)

            def copy_h(i):
                act.wait_ge(l1_done, i + 1)
                reached(act, ht_done, i)
                act.activation(h_sb[:, 0:512], HP[:, 0, :], ACT.Copy).then_inc(h_act, 1)

            def relu_h(i):
                act.wait_ge(hpre_ready, i + 1)
                reached(act, l2_done, i)
                act.activation(hT.rearrange("p m t -> p (m t)"), c_sb[:], ACT.Relu).then_inc(hT_ready, 1)

            def gate_y(i, u, j):
                act.wait_ge(yb_ready, i + 1)
                act.wait_ge(metas_in[u], 16 * (j + 1))
                act.activation(y[:, u, :], yb[:], ACT.Copy,
                               scale=meta_s[:, u, 1:2].bitcast(F32)).then_inc(y_ready, 1)

            def tile_body(j, first, last):
                for u in range(UB):
                    i = UB * j + u
                    copy_h(i)
                    if not (first and u == 0):
                        gate_y(i - 1, (u - 1) % UB, j if u else j - 1)
                    if not (last and u == UB - 1):
                        copy_x(i + 1)
                    relu_h(i)

            copy_x(0)
            tile_body(0, True, False)
            with act.Fori(1, TILES // UB - 1) as j:
                tile_body(j, False, False)
            tile_body(TILES // UB - 1, False, True)
            gate_y(TILES - 1, UB - 1, TILES // UB - 1)

        @block.gpsimd
        def _(pool):
            pool.memset(v33[:], 1.0).then_inc(setup_pool, 1)
            pool.memset(zeros[:], 0.0).then_inc(setup_pool, 1)
            pool.memset(m_sb[:], 0.0).then_inc(setup_pool, 1)
            step = Count(pool_step)

            def power(dst, src, n, var_sem, rstd_sem, value):
                pool.wait_ge(var_sem, value)
                pool.tensor_tensor(dst[:], src[:], half[:, 0:n], ALU.pow).then_inc(rstd_sem, 1)

            def copy_v(i, u, loads):
                pool_waits(pool, step, (ctx_in_s[u], loads), (pv_done, i - 1))
                pool.tensor_copy(v33[:, u, :, 0:DH],
                                 ctx_sb[:, u, :].rearrange("p (h d) -> p h d", h=NH)).then_inc(v33_ready, 1)

            def causal(b):
                pool_waits(pool, step, (arg_ready, b + 1))
                pool.affine_select(out=d_sb[:].rearrange("p (h s) -> p h s", h=NH),
                                   in_=d_sb[:].rearrange("p (h s) -> p h s", h=NH),
                                   pattern=[[0, NH], [1, S]], compare_op=ALU.is_ge, fill=NEG,
                                   base=0, channel_multiplier=-1).then_inc(masked, 1)

            def residual(b, u, stored):
                pool.wait_ge(hn_ready, b + 1)
                reached(pool, rows_out[u], stored)
                step.inc(pool.tensor_tensor(xr[:, u, :], hn[:].rearrange("p h d -> p (h d)"), normg[:], ALU.mult))
                step.wait(pool)
                pool.tensor_tensor(xr[:, u, :], xr[:, u, :],
                                   x_all[:, bass.ds(b % 4, 1), :].rearrange("p a c -> p (a c)"),
                                   ALU.add).then_inc(xr_ready, 1)

            def send_slots(p):
                pool_waits(pool, step, (slots_ready, p + 1))
                for q in range(4):
                    pool.indirect_dma_start(
                        meta_tab, bass.IndirectOffsetOnAxis(slot_i[:].bitcast(U32)[:, q:q + 1], 0),
                        meta[:, q, :], None, bounds_check=SLOTS - 1, oob_is_err=False).then_inc(slots_sent, 16)

            def body(j, f):
                i = 2 * j
                front, d0, d1, ra, rb = f["front"], f["d0"], f["d1"], f["ra"], f["rb"]
                if d0:
                    causal(i - 1)
                if front:
                    power(rstd, vare, 1, var_x, rstd_x, i + 1)
                    copy_v(i, 0, 16 * (j + 1))
                if d0:
                    power(rs, vs, 8, var_h, rstd_h, i)
                    residual(i - 1, 1, 32 * (j - 1))
                    power(rstd, vare, 1, var_r, rstd_r, i)
                if d1:
                    causal(i)
                if front:
                    power(rstd, vare, 1, var_x, rstd_x, i + 2)
                    copy_v(i + 1, 1, 16 * (j + 1))
                if rb:
                    send_slots(j - 2)
                if d1:
                    power(rs, vs, 8, var_h, rstd_h, i + 1)
                    residual(i, 0, 32 * j)
                    power(rstd, vare, 1, var_r, rstd_r, i + 1)

            pool.memset(half[:], -0.5).then_inc(setup_pool, 1)
            pool.wait_ge(setup_pool, 4)
            pool.wait_ge(setup_dve, 1)
            pool.wait_ge(tables_init, 48)
            run_bodies(pool, body, step)

            pool.wait_ge(slots_sent, 16 * 4 * (NB // 2))
            for u in range(2):
                pool.wait_ge(rows_out[u], 32 * (NB // 2))

            def gather(i, u, j):
                pool_waits(pool, step, (metag_in[u], 16 * (j + 1)), (xt_done, i - 2))
                pool.indirect_dma_start(xg[:, u, :], None, xf_tab,
                                        bass.IndirectOffsetOnAxis(meta_g[:, u, 0:1].bitcast(U32), 0),
                                        bounds_check=N + P - 1, oob_is_err=True).then_inc(gathered[u], 16)

            def scatter(i, u, j):
                v, jj = (u - 1) % UB, (j if u else j - 1)
                pool_waits(pool, step, (y_ready, i + 1), (scattered[v], 16 * (jj + 1)))
                pool.indirect_dma_start(out, bass.IndirectOffsetOnAxis(meta_s[:, u, 0:1].bitcast(U32), 0),
                                        y[:, u, :], None, bounds_check=N + P - 1, oob_is_err=True,
                                        compute_op=ALU.add).then_inc(scattered[u], 16)

            def tile_body(j, first, last):
                for u in range(UB):
                    i = UB * j + u
                    if not (last and u >= UB - 2):
                        gather(i + 2, (u + 2) % UB, j + (u + 2) // UB)
                    if not (first and u == 0):
                        scatter(i - 1, (u - 1) % UB, j if u else j - 1)
                step.restart(pool)

            gather(0, 0, 0)
            gather(1, 1, 0)
            step.restart(pool)
            tile_body(0, True, False)
            with pool.Fori(1, TILES // UB - 1) as j:
                tile_body(j, False, False)
            tile_body(TILES // UB - 1, False, True)
            scatter(TILES - 1, UB - 1, TILES // UB - 1)


def run_bodies(eng, body, steps=None):
    lo, hi = FULL

    def with_flags(j):
        f = flags(j)
        f["more"] = j + 1 < NB // 2
        return f

    def run(j, f):
        body(j, f)
        if steps:
            steps.restart(eng)

    if steps:
        steps.restart(eng)
    for j in range(lo):
        run(j, with_flags(j))
    full = with_flags(lo)
    with eng.Fori(lo, hi - 1) as j:
        run(j, full)
    for j in range(hi - 1, BODIES):
        run(j, with_flags(j))


_INS = ["x", "ctx_1024", "g_xattn", "g_ffn", "wg", "gb", "L0_xattn_norm_w", "L0_ffn_rw1", "rb1t",
        "L0_ffn_rw2", "L0_ffn_rb2", "L0_ffn_ew1", "eb1t", "L0_ffn_ew2", "L0_ffn_eb2",
        "cst", "tri", "tokids", "meta_init"]


def kernel(**inputs):
    import numpy as _np
    import ml_dtypes
    import concourse.bacc as _bacc
    from concourse import mybir as _mybir
    from concourse.bass_utils import run_bass_kernel_spmd as _run

    a = {k: _np.asarray(v) for k, v in inputs.items()}
    order = [(hh % 2) * 4 + hh // 2 for hh in range(NH)]
    w = _np.concatenate([a["L0_xattn_igate_w"][order], a["L0_xattn_fgate_w"][order]])
    a["wg"] = w.reshape(2 * NH, 6, P).transpose(2, 1, 0)
    a["gb"] = _np.concatenate([a["L0_xattn_igate_b"][order], a["L0_xattn_fgate_b"][order]])
    a["rb1t"] = a["L0_ffn_rb1"].reshape(KH, P).T
    a["eb1t"] = a["L0_ffn_eb1"].reshape(NE, KH, P).transpose(2, 0, 1)
    cst = _np.zeros((P, 320), _np.float32)
    cst[:, 0:P] = _np.eye(P)
    cst[:, P:2 * P] = _np.triu(_np.ones((P, P)))
    cst[:, 256:264] = _np.arange(NE)
    cst[:, 264:272] = _np.arange(8) * P
    cst[:, 272:280] = _np.arange(NE) * CAP
    cst[:, 280:280 + TILES] = _np.arange(TILES)
    a["cst"] = cst
    tri = _np.ones((P, 2, P), _np.float32)
    tri[:, 0, :] = _np.triu(_np.ones((P, P)), 1)
    a["tri"] = tri.astype(ml_dtypes.bfloat16)
    a["tokids"] = (_np.arange(NB)[None, :] * P + _np.arange(P)[:, None]).astype(_np.int32)
    meta_init = _np.zeros((SLOTS + P, 2), _np.int32)
    meta_init[:, 0] = N + _np.arange(SLOTS + P) % P
    a["meta_init"] = meta_init

    nc = _bacc.Bacc("TRN2", target_bir_lowering=False, num_devices=1)
    arrays, args = {}, []
    for name in _INS:
        v = _np.ascontiguousarray(a[name])
        arrays[f"in_{name}_dram"] = v
        args.append(nc.dram_tensor(f"in_{name}_dram", v.shape, _mybir.dt.from_np(v.dtype), kind="ExternalInput").ap())
    out = nc.dram_tensor("out_0_dram", (N + P, C), _mybir.dt.float32, kind="ExternalOutput").ap()
    build(nc, *args, out)
    r = _run(nc, [arrays], core_ids=[0])
    return _np.asarray(r.results[0]["out_0_dram"])[0:N].reshape(NB, S, C)
```

```python
from contextlib import ExitStack

import numpy as np
import concourse.bass as bass
from concourse import mybir

ALU = mybir.AluOpType
ACT = mybir.ActivationFunctionType
AXX = mybir.AxisListType.X
F32 = mybir.dt.float32
BF16 = mybir.dt.bfloat16
I32 = mybir.dt.int32
U32 = mybir.dt.uint32

P = 128
NB, S, C = 16, 128, 256
NH, DH = 8, 32
N = NB * S
H = 1024
NE, TOPK, CAP = 8, 2, 1024
KC = C // P
KH = H // P
PAIRS = NB // 2
TILES = (N * TOPK + NE * (P - 1)) // P
SLOTS = NE * CAP
EMPTY_ROW = SLOTS
UB = 3
assert TILES % UB == 0 and NB % 4 == 0 and PAIRS == NE
EPS_LN, EPS_DEN = 1e-5, 1e-6
SCALE = float(DH) ** -0.5
NEG = -1.0e30


class Count:

    def __init__(self, sem):
        self.sem, self.n = sem, 0

    def inc(self, ins):
        ins.then_inc(self.sem, 1)
        self.n += 1

    def wait(self, eng):
        if self.n:
            eng.wait_ge(self.sem, self.n)

    def restart(self, eng):
        self.wait(eng)
        eng.sem_clear(self.sem)
        self.n = 0


def reached(eng, sem, value):
    if isinstance(value, int) and value <= 0:
        return
    eng.wait_ge(sem, value)


def flags(j):
    return dict(att=j < PAIRS, fin=1 <= j <= PAIRS, rt=2 <= j <= PAIRS + 1, ch=3 <= j <= PAIRS + 2,
                more=j + 1 < PAIRS)


BODIES = PAIRS + 3
FULL = (4, PAIRS)
GB = 4


def build(nc, x, ctx_in, g_x, g_f, wg, gb, norm_w, rw1, rb1t, rw2, rb2, ew1, eb1t, ew2, eb2,
          cst, tri_in, tokids, meta_init, out):
    def dram(name, shape, dt):
        return nc.dram_tensor(name, shape, dt, kind="Internal").ap()

    m_dram = dram("m_dram", (NB, NH * S), F32)
    xf_tab = dram("xf_tab", (N + P, C), F32)
    meta_tab = dram("meta_tab", (SLOTS + P, 2), I32)

    with ExitStack() as stack:
        def sb(name, shape, dt=F32):
            return stack.enter_context(nc.sbuf_tensor(name, shape, dt))

        def sem(name):
            return stack.enter_context(nc.semaphore(name))

        ps = stack.enter_context(nc.psum_tensor("ps", [P, 8, 512], F32))

        cst_sb = sb("cst_sb", [P, 320])
        ident = cst_sb[:, 0:P]
        triu_incl = cst_sb[:, P:2 * P]
        iota_e = cst_sb[:, 256:256 + NE]
        blk_thr = cst_sb[0:1, 264:272]
        exp_row = cst_sb[0:1, 272:280]
        tile_id = cst_sb[0:1, 280:280 + TILES]
        tri = sb("tri", [P, 2, P], BF16)
        tok_sb = sb("tok_sb", [P, NB], I32)
        w_gate = sb("w_gate", [P, 6, 16])
        w_gc = sb("w_gc", [P, 4, 16])
        gate_b = sb("gate_b", [P, 16])
        norm_sb = sb("norm_sb", [P, C])
        normg = sb("normg", [P, C])
        g2 = sb("g2", [P, 2])
        tg = sb("tg", [P, 2])
        rw1_sb = sb("rw1_sb", [P, KC, H])
        rb1_sb = sb("rb1_sb", [P, KH])
        rw2_sb = sb("rw2_sb", [P, KH, NE])
        rb2_sb = sb("rb2_sb", [NE, 1])
        w1 = sb("w1", [P, NE, KC, H])
        w2 = sb("w2", [P, NE, KH, C])
        b1 = sb("b1", [P, NE, KH])
        b2 = sb("b2", [P, NE, C])
        zeros = sb("zeros", [P, C])

        stats = sb("stats", [P, GB, 6])
        mv = sb("mv", [P, GB, 2])
        spare = sb("spare", [P, 1])
        vare = sb("vare", [P, GB])
        rstd = sb("rstd", [P, GB])
        half = sb("half", [P, 16])
        gts = sb("gts", [P, NB, 16])
        nab = sb("nab", [P, NB, 8])
        ex = sb("ex", [P, NB, 8])
        lp = sb("lp", [P, NB, 8])
        lf = sb("lf", [P, NB, 8])
        fcum = sb("fcum", [P, NB * 8])
        a_sb = sb("a_sb", [P, NB, 8])
        m_sb = sb("m_sb", [P, P])
        fm = sb("fm", [P, NB, 8])
        nm = sb("nm", [P, NB, 8])

        m_bc = sb("m_bc", [P, 2, NH * S])
        d_sb = sb("d_sb", [P, 2, NH * S])
        c_sb = sb("c_sb", [P, NH * S])
        v33 = sb("v33", [P, 2, NH, DH + 1])
        o_sb = sb("o_sb", [P, 2, NH, DH + 1])
        nrm = sb("nrm", [P, 16])
        den = sb("den", [P, 16])
        hv = sb("hv", [P, 16, DH])
        sm = sb("sm", [P, 16])
        hc = sb("hc", [P, 16, DH])
        vs = sb("vs", [P, 16])
        vh = sb("vh", [P, 16])
        rs = sb("rs", [P, 16])
        hn = sb("hn", [P, 16, DH])
        xr = sb("xr", [P, 2, C])
        xf = sb("xf", [P, 2, C])
        xfT = sb("xfT", [P, KC, 2 * P])
        hbuf = sb("hbuf", [P, KH, 2 * P])
        lgT = sb("lgT", [P, 2, P])
        lg = sb("lg", [P, 2, NE])
        mx = sb("mx", [P, 2, 8])
        mi = sb("mi", [P, 2, 8], U32)
        mif = sb("mif", [P, 2, 2])
        dd = sb("dd", [P, 2, 1])
        ee = sb("ee", [P, 2, 1])
        s1 = sb("s1", [P, 2, 1])
        pr = sb("pr", [P, 2, 2])
        oh = sb("oh", [P, 2, 2, NE])
        mask = sb("mask", [P, 2, NE], BF16)
        before = sb("before", [P, 2, NE], BF16)
        pm = sb("pm", [P, 2, 2, NE])
        pos = sb("pos", [P, 2, 2])
        over = sb("over", [P, 2, 2])
        slot = sb("slot", [P, 2, 2])
        slot_i = sb("slot_i", [P, 4], I32)
        meta = sb("meta", [P, 4, 2], I32)
        qk = sb("qk", [P, 2, 4, P])
        xn = c_sb[:].rearrange("p (u c) -> p u c", u=GB)
        gT = d_sb[0:16].rearrange("p a n -> p (a n)").rearrange("p (g n) -> p g n", g=NB // GB)

        cnt = sb("cnt", [1, NE])
        blk = sb("blk", [1, NE, 8])
        nblk = sb("nblk", [1, NE])
        ones_r = sb("ones_r", [1, NE])
        end = sb("end", [1, NE])
        start = sb("start", [1, NE])
        base = sb("base", [1, NE])
        ge, gs, inr, rowc = (m_bc[0:1, k, q * 512:q * 512 + TILES * NE].rearrange("p (t e) -> p t e", e=NE)
                             for k, q in ((0, 0), (0, 1), (1, 0), (1, 1)))
        eidx = sb("eidx", [1, TILES])
        rsum = sb("rsum", [1, TILES])
        emp = sb("emp", [1, TILES])
        sched_row = sb("sched_row", [1, TILES], I32)
        sched_e = sb("sched_e", [1, TILES], I32)

        meta_g = sb("meta_g", [P, UB, 2], I32)
        meta_s = sb("meta_s", [P, UB, 2], I32)
        xg = d_sb[:, 0, 0:UB * C].rearrange("p (u c) -> p u c", u=UB)
        xT = hc[:, 0:8, :].rearrange("p (k a) d -> p k (a d)", k=KC)
        h_sb = hbuf[:, 0:4, :].rearrange("p m t -> p (m t)")
        hT = hbuf[:, 4:8, :].rearrange("p m t -> p (m t)").rearrange("p (m t) -> p m t", m=KH)
        hpre = c_sb[:, :].rearrange("p (m t) -> p m t", m=KH)
        yb = hn[:, 0:8, :].rearrange("p h d -> p (h d)")
        y = d_sb[:, 1, 0:UB * C].rearrange("p (u c) -> p u c", u=UB)

        S4 = ps[:, 0:4, 0:256]
        O2 = ps[:, 0:2, 256:256 + 4 * (DH + 1)]
        O4 = O2.rearrange("p g (j d) -> p g j d", j=4)
        LGT = ps[0:NE, 7, 0:2 * P]
        LGX = ps[:, 7, 2 * P:4 * P].rearrange("p (b t) -> p b t", b=2)
        LG = LGX[:, :, 0:NE]
        PFX = ps[:, 4, 0:2 * NE].rearrange("p (b e) -> p b e", b=2)
        CNT = ps[:, 4, 0:NE]
        T4 = ps[:, 4, :].rearrange("p (c t) -> p c t", c=4)
        GTS = ps[:, 6, 0:NB * 16].rearrange("p (b n) -> p b n", b=NB)
        FC = ps[:, 5, 0:P]
        AT = ps[:, 4, 0:P]
        MT = ps[:, 7, 0:P]

        def RH(m):
            return ps[:, 5 + m % 2, 0:2 * P]

        def w2_row(p, m):
            return w2[:, bass.ds(p, 1), m, :].rearrange("p a c -> p (a c)")

        def ctx_of(p, u):
            return w2_row(p, 2 + u)

        def qk_of(p, u):
            return w2[:, bass.ds(p, 1), 4 + 2 * u:6 + 2 * u, :].rearrange("p a m c -> p (a m c)")

        def qk_chunk(g, c):
            return (w2[:, 2 * g:2 * g + 2, 4:8, :]
                    .rearrange("p a (u k) (d t) -> p a u k d t", u=2, d=2)[:, :, :, c // 2, c % 2, :])

        HP = ps[:, 0:2, :]
        HT = ps[:, 2:4, :].rearrange("p b (m t) -> p (b m) t", m=4)
        YP = ps[:, 4, 0:C]
        XT = ps[:, 5, 0:KC * P].rearrange("p (c t) -> p c t", c=KC)

        cst_in = sem("cst_in")
        late_in = sem("late_in")
        tables_init = sem("tables_init")
        weights_in = sem("weights_in")
        x_in = [sem(f"x_in{g}") for g in range(NB // GB)]
        qk_in = [sem(f"qk_in{u}") for u in range(2)]
        ctx_in_s = [sem(f"ctx_in{g}") for g in range(NB // GB)]
        setup_dve = sem("setup_dve")
        setup_pool = sem("setup_pool")
        tanh_ready = sem("tanh_ready")
        xn_ready = sem("xn_ready")
        t_done = sem("t_done")
        qkT_ready = sem("qkT_ready")
        v33_ready = sem("v33_ready")
        gates_done = sem("gates_done")
        gT_ready = sem("gT_ready")
        gts_done = sem("gts_done")
        gts_ready = sem("gts_ready")
        nab_ready = sem("nab_ready")
        ex_ready = sem("ex_ready")
        lp_ready = sem("lp_ready")
        lf_ready = sem("lf_ready")
        f_done = sem("f_done")
        a_ready = sem("a_ready")
        at_done = sem("at_done")
        m_ready = sem("m_ready")
        m_stored = sem("m_stored")
        m_bc_in = [sem(f"m_bc_in{u}") for u in range(2)]
        mt_done = sem("mt_done")
        fm_ready = sem("fm_ready")
        nm_ready = sem("nm_ready")
        nme_ready = sem("nme_ready")
        s_done = sem("s_done")
        arg_ready = sem("arg_ready")
        masked = sem("masked")
        d_ready = sem("d_ready")
        c_ready = sem("c_ready")
        pv_done = sem("pv_done")
        o_ready = sem("o_ready")
        o_used = sem("o_used")
        hc_ready = sem("hc_ready")
        sq_ready = sem("sq_ready")
        hn_ready = sem("hn_ready")
        pool_step = sem("pool_step")
        xr_ready = sem("xr_ready")
        xf_ready = sem("xf_ready")
        rows_out = sem("rows_out")
        xf_t_done = sem("xf_t_done")
        xfT_ready = sem("xfT_ready")
        rh_done = sem("rh_done")
        rh_ready = sem("rh_ready")
        lgT_done = sem("lgT_done")
        lgT_ready = sem("lgT_ready")
        lg_done = sem("lg_done")
        diff_ready = sem("diff_ready")
        ee_ready = sem("ee_ready")
        mask_ready = sem("mask_ready")
        pfx_done = sem("pfx_done")
        pfx_read = sem("pfx_read")
        slots_ready = sem("slots_ready")
        slots_sent = sem("slots_sent")
        cnt_done = sem("cnt_done")
        sched_ready = sem("sched_ready")
        var_x, rstd_x = sem("var_x"), sem("rstd_x")
        var_h, rstd_h = sem("var_h"), sem("rstd_h")
        var_r, rstd_r = sem("var_r"), sem("rstd_r")
        dve_step = sem("dve_step")
        act_step = sem("act_step")

        metag_in = [sem(f"metag_in{u}") for u in range(UB)]
        metas_in = [sem(f"metas_in{u}") for u in range(UB)]
        gathered = [sem(f"gathered{u}") for u in range(UB)]
        scattered = [sem(f"scattered{u}") for u in range(UB)]
        xt_done = sem("xt_done")
        xT_ready = sem("xT_ready")
        l1_done = sem("l1_done")
        h_act = sem("h_act")
        h_dve = sem("h_dve")
        ht_done = sem("ht_done")
        hpre_ready = sem("hpre_ready")
        hT_ready = sem("hT_ready")
        l2_done = sem("l2_done")
        yb_ready = sem("yb_ready")
        y_ready = sem("y_ready")

        N_CST, N_LATE = 6, 8
        block = stack.enter_context(nc.Block())

        def consts(eng):
            eng.wait_ge(cst_in, 16 * N_CST)

        def late_consts(eng):
            eng.wait_ge(late_in, 16 * N_LATE)

        def pool_waits(pool, step, *conditions):
            step.wait(pool)
            for sm_, v in conditions:
                reached(pool, sm_, v)
            step.inc(pool.tensor_tensor(spare[:], half[:, 0:1], half[:, 0:1], ALU.add))
            pool.wait_ge(setup_pool, 4)
            for sm_, v in conditions:
                reached(pool, sm_, v)

        @block.sync
        def _(sp):
            def load_group(g):
                for p in (2 * g, 2 * g + 1):
                    for src, m, s in ((ctx_in, 2, ctx_in_s[g]), (x, 0, x_in[g])):
                        sp.dma_start(w2[:, p, m:m + 2, :],
                                     src[2 * p:2 * p + 2, :, :].rearrange("b p c -> p b c")).then_inc(s, 16)

            load_group(0)
            for dst, src in ((cst_sb, cst), (w_gate, wg), (gate_b, gb.partition_broadcast(P)),
                             (norm_sb, norm_w.partition_broadcast(P))):
                sp.dma_start(dst[:], src).then_inc(cst_in, 16)
            sp.dma_start(g2[:, 0:1], g_x.partition_broadcast(P)).then_inc(cst_in, 16)
            sp.dma_start(g2[:, 1:2], g_f.partition_broadcast(P)).then_inc(cst_in, 16)
            for g in range(1, NB // GB):
                load_group(g)
            for dst, src in ((tok_sb, tokids), (rb1_sb, rb1t), (rw2_sb, rw2.rearrange("(m p) e -> p m e", p=P)),
                             (rb2_sb, rb2.unsqueeze(1)), (b1, eb1t), (tri, tri_in),
                             (rw1_sb, rw1.rearrange("(k p) h -> p k h", p=P))):
                sp.dma_start(dst[:], src).then_inc(late_in, 16)
            sp.dma_start(b2[:].rearrange("p e c -> p (e c)"),
                         eb2.rearrange("e c -> (e c)").partition_broadcast(P)).then_inc(late_in, 16)
            sp.dma_start(meta_tab, meta_init).then_inc(tables_init, 16)
            sp.wait_ge(setup_pool, 2)
            sp.dma_start(xf_tab[N:N + P, :], zeros[:]).then_inc(tables_init, 16)
            sp.dma_start(out[N:N + P, :], zeros[:]).then_inc(tables_init, 16)

            def load_qk(b, p, u):
                sp.dma_start(qk[:, u, :, :].rearrange("p c t -> p (c t)"), qk_of(p, u)).then_inc(qk_in[u], 16)

            def load_m(b, u):
                sp.dma_start(m_bc[:, u, :],
                             m_dram[bass.ds(b, 1), :].rearrange("a n -> (a n)").partition_broadcast(P)
                             ).then_inc(m_bc_in[u], 16)

            sp.wait_ge(m_ready, 1)
            sp.dma_start(m_dram.rearrange("b (h s) -> (b h) s", h=NH), m_sb[:]).then_inc(m_stored, 16)
            sp.wait_ge(qkT_ready, NB)
            for u in range(2):
                load_qk(u, 0, u)
            sp.wait_ge(m_stored, 16)
            for u in range(2):
                load_m(u, u)

            def body(j, f):
                if f["more"]:
                    for u in range(2):
                        sp.wait_ge(arg_ready, 2 * j + u + 1)
                        load_m(2 * j + 2 + u, u)
                        sp.wait_ge(s_done, 2 * j + u + 1)
                        load_qk(2 * j + 2 + u, j + 1, u)
                if f["att"]:
                    sp.dma_start(w1[:, bass.ds(j, 1), :, :].rearrange("p a k h -> p (a k) h"),
                                 ew1[bass.ds(j, 1), :, :].rearrange("a (k p) h -> p (a k) h", p=P)
                                 ).then_inc(weights_in, 16)
                if f["fin"]:
                    p = j - 1
                    sp.wait_ge(xf_ready, p + 1)
                    sp.dma_start(out[bass.ds(p * 2 * P, 2 * P), :].rearrange("(b p) c -> p b c", p=P),
                                 xr[:]).then_inc(rows_out, 16)
                    sp.dma_start(xf_tab[bass.ds(p * 2 * P, 2 * P), :].rearrange("(b p) c -> p b c", p=P),
                                 xf[:]).then_inc(rows_out, 16)
                    sp.dma_start(w2[:, bass.ds(p, 1), :, :].rearrange("p a m c -> p (a m) c"),
                                 ew2[bass.ds(p, 1), :, :].rearrange("a (m p) c -> p (a m) c", p=P)
                                 ).then_inc(weights_in, 16)

            run_bodies(sp, body)

            sp.wait_ge(sched_ready, 1)
            sp.wait_ge(slots_sent, 16 * 4 * (NB // 2))

            def load_meta(row, u, dst, s):
                sp.dma_start(dst[:, u, :], meta_tab[bass.ds(row, P), :]).then_inc(s, 16)

            def tile_body(j, first):
                for u in range(UB):
                    row = sp.value_load(sched_row[0:1, bass.ds(UB * j + u, 1)], min_val=0, max_val=SLOTS)
                    if not first:
                        sp.wait_ge(gathered[u], 16 * j)
                    load_meta(row, u, meta_g, metag_in[u])
                    if not first:
                        sp.wait_ge(scattered[u], 16 * j)
                    load_meta(row, u, meta_s, metas_in[u])

            tile_body(0, True)
            with sp.Fori(1, TILES // UB) as j:
                tile_body(j, False)
            for u in range(UB):
                sp.wait_ge(scattered[u], 16 * (TILES // UB))
                sp.wait_ge(metas_in[u], 16 * (TILES // UB))
            sp.wait_ge(rows_out, 32 * PAIRS)

        @block.tensor
        def _(pe):
            def transposes_T(g, c):
                if c < 2:
                    pe.wait_ge(xn_ready, GB * (g + 1))
                else:
                    pe.wait_ge(ctx_in_s[g], 32)
                reached(pe, qkT_ready, 4 * (g - 1) + (c + 2) % 4 + 1)
                for u in range(GB):
                    src = xn[:, u, :] if c < 2 else w2[:, 2 * g + u // 2, 2 + u % 2, :]
                    ins = pe.transpose(ps[:, c, u * P:(u + 1) * P], src[:, c % 2 * P:(c % 2 + 1) * P], ident[:])
                ins.then_inc(t_done, 1)

            def gates(g):
                reached(pe, gT_ready, g - 1)
                for n, c in enumerate((2, 3, 0, 1)):
                    pe.wait_ge(qkT_ready, 4 * g + n + 1)
                    ins = pe.matmul(ps[0:16, 4 + g % 2, :], w_gc[:, c, :], qk_chunk(g, c),
                                    start=(n == 0), stop=(n == 3))
                ins.then_inc(gates_done, 1)

            def gates_back(g):
                pe.wait_ge(gT_ready, g + 1)
                for u in range(GB):
                    ins = pe.transpose(GTS[:, GB * g + u, :], gT[:, g, u * P:(u + 1) * P], ident[0:16, 0:16])
                return ins

            def scores(b, p, u):
                pe.wait_ge(qk_in[u], 16 * (p + 1))
                reached(pe, o_ready, b)
                for g in range(2):
                    for r in range(4):
                        rows = slice(DH * r, DH * (r + 1))
                        ins = pe.matmul(S4[:, r, g * P:(g + 1) * P], qk[rows, u, 2 + g, :], qk[rows, u, g, :],
                                        start=True, stop=True, tile_position=(DH * r, 0))
                ins.then_inc(s_done, 1)

            def pv(b, u):
                pe.wait_ge(c_ready, b + 1)
                pe.wait_ge(v33_ready, b + 1)
                for h in range(NH):
                    hh = (h % 4) * 2 + h // 4
                    ins = pe.matmul(O4[:, h // 4, h % 4, :], c_sb[:, hh * P:(hh + 1) * P], v33[:, u, h, :],
                                    start=True, stop=True)
                ins.then_inc(pv_done, 1)

            def router_T(p):
                pe.wait_ge(xf_ready, p + 1)
                reached(pe, pfx_read, p - 1)
                for b in range(2):
                    for c in range(2):
                        ins = pe.transpose(T4[:, 2 * c + b, :], xf[:, b, c * P:(c + 1) * P], ident[:])
                ins.then_inc(xf_t_done, 1)

            def router_hidden(p, m):
                pe.wait_ge(xfT_ready, p + 1)
                reached(pe, rh_ready, KH * p + m - 1)
                for k in range(KC):
                    ins = pe.matmul(RH(m), rw1_sb[:, k, m * P:(m + 1) * P], xfT[:, k, :],
                                    start=(k == 0), stop=(k == KC - 1))
                ins.then_inc(rh_done, 1)

            def router_logits(p, half_of):
                if half_of == 0:
                    pe.wait_ge(rh_ready, KH * (p + 1))
                    reached(pe, mask_ready, p)
                for m in range(4 * half_of, 4 * half_of + 4):
                    ins = pe.matmul(LGT, rw2_sb[:, m, :], hbuf[:, m, :], start=(m == 0), stop=(m == KH - 1))
                if half_of:
                    ins.then_inc(lgT_done, 1)

            def logits_back(p):
                pe.wait_ge(lgT_ready, p + 1)
                for b in range(2):
                    ins = pe.transpose(LGX[:, b, :], lgT[:, b, :], ident[:])
                ins.then_inc(lg_done, 1)

            def prefix(p):
                pe.wait_ge(mask_ready, p + 1)
                for b in range(2):
                    pe.matmul(PFX[:, b, :], tri[:, 0, :], mask[:, b, :], start=True, stop=False)
                    ins = pe.matmul(PFX[:, b, :], tri[:, 1, :], before[:, b, :], start=False, stop=True)
                ins.then_inc(pfx_done, 1)

            def body(j, f):
                att, rt = f["att"], f["rt"]

                def hidden(*chunks):
                    if rt:
                        for m in chunks:
                            router_hidden(j - 2, m)

                if att:
                    scores(2 * j, j, 0)
                if f["ch"]:
                    router_logits(j - 3, 0)
                if rt:
                    router_T(j - 2)
                if f["ch"]:
                    router_logits(j - 3, 1)
                hidden(0)
                if f["ch"]:
                    logits_back(j - 3)
                hidden(1)
                if att:
                    pv(2 * j, 0)
                hidden(2, 3)
                if att:
                    scores(2 * j + 1, j, 1)
                hidden(4, 5)
                if att:
                    pv(2 * j + 1, 1)
                if f["ch"]:
                    prefix(j - 3)
                hidden(6, 7)

            consts(pe)
            pe.wait_ge(setup_dve, 1)
            for g in range(NB // GB):
                for c in (2, 3, 0, 1):
                    transposes_T(g, c)
                if g:
                    gates_back(g - 1)
                gates(g)
            gates_back(NB // GB - 1).then_inc(gts_done, 1)
            pe.wait_ge(lf_ready, 1)
            pe.matmul(FC, triu_incl[:], lf[:].rearrange("p b h -> p (b h)"), start=True, stop=True).then_inc(f_done, 1)
            pe.wait_ge(a_ready, 1)
            pe.transpose(AT, a_sb[:].rearrange("p b h -> p (b h)"), ident[:]).then_inc(at_done, 1)
            pe.wait_ge(m_ready, 1)
            pe.transpose(MT, m_sb[:], ident[:]).then_inc(mt_done, 1)
            pe.wait_ge(fm_ready, 1)
            late_consts(pe)
            run_bodies(pe, body)

            pe.wait_ge(pfx_read, NB // 2)
            pe.matmul(CNT, tri[:, 1, :], before[:, 0, :], start=True, stop=True).then_inc(cnt_done, 1)

            pe.wait_ge(sched_ready, 1)
            pe.wait_ge(weights_in, 32 * NE)

            def expert(i):
                return pe.value_load(sched_e[0:1, bass.ds(i, 1)], min_val=0, max_val=NE - 1)

            def x_transpose(i, u, j):
                pe.wait_ge(gathered[u], 16 * (j + 1))
                reached(pe, xT_ready, i)
                for c in range(KC):
                    ins = pe.transpose(XT[:, c, :], xg[:, u, c * P:(c + 1) * P], ident[:])
                ins.then_inc(xt_done, 1)

            def layer1(i, e):
                pe.wait_ge(xT_ready, i + 1)
                reached(pe, h_act, i)
                reached(pe, h_dve, i)
                for n in range(2):
                    for k in range(KC):
                        ins = pe.matmul(HP[:, n, :], xT[:, k, :],
                                        w1[:, bass.ds(e, 1), k, n * 512:(n + 1) * 512].rearrange("p a n -> p (a n)"),
                                        start=(k == 0), stop=(k == KC - 1))
                ins.then_inc(l1_done, 1)

            def h_transpose(i):
                pe.wait_ge(h_act, i + 1)
                pe.wait_ge(h_dve, i + 1)
                reached(pe, hpre_ready, i)
                for m in range(KH):
                    ins = pe.transpose(HT[:, m, :], h_sb[:, m * P:(m + 1) * P], ident[:])
                ins.then_inc(ht_done, 1)

            def layer2(i, e):
                pe.wait_ge(hT_ready, i + 1)
                reached(pe, yb_ready, i)
                for m in range(KH):
                    ins = pe.matmul(YP, hT[:, m, :],
                                    w2[:, bass.ds(e, 1), m, :].rearrange("p a n -> p (a n)"),
                                    start=(m == 0), stop=(m == KH - 1))
                ins.then_inc(l2_done, 1)

            def tile_body(j, first, last):
                for u in range(UB):
                    i = UB * j + u
                    e = expert(i)
                    layer1(i, e)
                    if not (last and u == UB - 1):
                        x_transpose(i + 1, (u + 1) % UB, j + (u + 1) // UB)
                    if not (first and u == 0):
                        layer2(i - 1, expert(i - 1))
                    h_transpose(i)

            x_transpose(0, 0, 0)
            tile_body(0, True, False)
            with pe.Fori(1, TILES // UB - 1) as j:
                tile_body(j, False, False)
            tile_body(TILES // UB - 1, False, True)
            layer2(TILES - 1, expert(TILES - 1))

        @block.vector
        def _(ve):
            chain = Count(dve_step)

            def link(ins):
                chain.inc(ins)
                chain.wait(ve)

            def both(first, second):
                chain.inc(first)
                link(second)

            def norm_group(g):
                ve.wait_ge(x_in[g], 32)

                def x_of(u):
                    return w2[:, 2 * g + u // 2, u % 2, :]

                for u in range(GB):
                    chain.inc(ve.bn_stats(stats[:, u, :], x_of(u)))
                chain.wait(ve)
                for u in range(GB):
                    chain.inc(ve.bn_aggr(mv[:, u, :], stats[:, u, :]))
                chain.wait(ve)
                ve.tensor_scalar(vare[:], mv[:, :, 1], EPS_LN, None, ALU.add).then_inc(var_x, 1)
                if g:
                    copy_gates(g - 1)
                ve.wait_ge(rstd_x, g + 1)
                reached(ve, t_done, 4 * g)
                for u in range(GB):
                    ve.tensor_scalar(xn[:, u, :], x_of(u), mv[:, u, 0:1],
                                     rstd[:, u:u + 1], ALU.subtract, ALU.mult).then_inc(xn_ready, 1)

            def copy_gates(g):
                ve.wait_ge(gates_done, g + 1)
                ve.tensor_copy(gT[:, g, :], ps[0:16, 4 + g % 2, :]).then_inc(gT_ready, 1)

            def gate_curves():
                ve.wait_ge(gts_done, 1)
                ve.tensor_tensor(gts[:], GTS, gate_b[:].unsqueeze(1).broadcast_to([P, NB, 16]),
                                 ALU.add).then_inc(gts_ready, 1)
                ve.wait_ge(gts_ready, 1)
                f_raw = gts[:, :, 8:16]
                ve.scalar_tensor_tensor(nab[:], f_raw, -1.0, f_raw, ALU.mult, ALU.min).then_inc(nab_ready, 1)
                ve.wait_ge(lp_ready, 1)
                ve.scalar_tensor_tensor(lf[:], f_raw, 0.0, lp[:], ALU.min, ALU.subtract).then_inc(lf_ready, 1)
                ve.wait_ge(f_done, 1)
                link(ve.tensor_copy(fcum[:], FC))
                ve.tensor_tensor(a_sb[:], gts[:, :, 0:8], fcum[:].rearrange("p (b h) -> p b h", b=NB),
                                 ALU.subtract).then_inc(a_ready, 1)
                ve.wait_ge(at_done, 1)
                ve.tensor_tensor_scan(m_sb[:], zeros[:, 0:P], AT, -3.0e38, ALU.add, ALU.max).then_inc(m_ready, 1)
                ve.wait_ge(mt_done, 1)
                ve.tensor_tensor(fm[:].rearrange("p b h -> p (b h)"), fcum[:], MT, ALU.add).then_inc(fm_ready, 1)
                ve.wait_ge(nm_ready, 1)
                ve.tensor_scalar(nm[:], nm[:], EPS_DEN, None, ALU.add).then_inc(nme_ready, 1)

            def decay_arg(b, u, loads):
                ve.wait_ge(m_bc_in[u], loads)
                reached(ve, c_ready, b - 1)
                ve.tensor_tensor(d_sb[:, u, :].rearrange("p (h s) -> p h s", h=NH),
                                 a_sb[:, bass.ds(b, 1), :].rearrange("p a h -> p (a h)").unsqueeze(2)
                                 .broadcast_to([P, NH, S]),
                                 m_bc[:, u, :].rearrange("p (h s) -> p h s", h=NH),
                                 ALU.subtract).then_inc(arg_ready, 1)

            def weigh(b, u):
                ve.wait_ge(s_done, b + 1)
                ve.wait_ge(d_ready, b + 1)
                reached(ve, pv_done, b)
                ve.scalar_tensor_tensor(c_sb[:].rearrange("p (r n) -> p r n", r=4), S4, SCALE,
                                        d_sb[:, u, :].rearrange("p (r n) -> p r n", r=4),
                                        ALU.mult, ALU.mult).then_inc(c_ready, 1)

            o_pair = o_sb[:].rearrange("p b h d -> p (b h) d")

            def over_d(a):
                return a.unsqueeze(2).broadcast_to([P, 16, DH])

            def normalise(p):
                ve.wait_ge(o_ready, 2 * (p + 1))
                rowsum = o_pair[:, :, DH]
                link(ve.scalar_tensor_tensor(nrm[:], rowsum, -1.0, rowsum, ALU.mult, ALU.max))
                link(ve.scalar_tensor_tensor(nrm[:], nrm[:], EPS_DEN,
                                             nm[:, bass.ds(2 * p, 2), :].rearrange("p b h -> p (b h)"),
                                             ALU.add, ALU.max))
                link(ve.reciprocal(den[:], nrm[:]))
                ve.tensor_tensor(hv[:], o_pair[:, :, 0:DH], over_d(den[:]), ALU.mult).then_inc(o_used, 1)
                ve.wait_ge(o_used, p + 1)
                link(ve.tensor_reduce(sm[:], hv[:], AXX, ALU.add))
                ve.scalar_tensor_tensor(hc[:], over_d(sm[:]), -1.0 / DH, hv[:],
                                        ALU.mult, ALU.add).then_inc(hc_ready, 1)

            def head_var(p):
                ve.wait_ge(sq_ready, p + 1)
                link(ve.tensor_reduce(vs[:], hv[:], AXX, ALU.add))
                ve.tensor_scalar(vh[:], vs[:], 1.0 / DH, EPS_LN, ALU.mult, ALU.add).then_inc(var_h, 1)

            def scale_heads(p):
                ve.wait_ge(rstd_h, p + 1)
                reached(ve, xr_ready, p)
                ve.tensor_tensor(hn[:], hc[:], over_d(rs[:]), ALU.mult).then_inc(hn_ready, 1)

            def res_var(p):
                ve.wait_ge(xr_ready, p + 1)
                both(ve.bn_stats(stats[:, 0, :], xr[:, 0, :]), ve.bn_stats(stats[:, 1, :], xr[:, 1, :]))
                both(ve.bn_aggr(mv[:, 0, :], stats[:, 0, :]), ve.bn_aggr(mv[:, 1, :], stats[:, 1, :]))
                ve.tensor_scalar(vare[:, 0:2], mv[:, 0:2, 1], EPS_LN, None, ALU.add).then_inc(var_r, 1)

            def norm_res(p):
                ve.wait_ge(rstd_r, p + 1)
                reached(ve, rows_out, 32 * p)
                reached(ve, xf_t_done, p)
                link(ve.tensor_scalar(xf[:, 0, :], xr[:, 0, :], mv[:, 0, 0:1], rstd[:, 0:1], ALU.subtract, ALU.mult))
                ve.tensor_scalar(xf[:, 1, :], xr[:, 1, :], mv[:, 1, 0:1], rstd[:, 1:2],
                                 ALU.subtract, ALU.mult).then_inc(xf_ready, 1)

            def choose(p):
                ve.wait_ge(lg_done, p + 1)
                link(ve.tensor_copy(lg[:], LG))
                both(ve.max(mx[:, 0, :], lg[:, 0, :]), ve.max(mx[:, 1, :], lg[:, 1, :]))
                both(ve.max_index(mi[:, 0, :], mx[:, 0, :], lg[:, 0, :]),
                     ve.max_index(mi[:, 1, :], mx[:, 1, :], lg[:, 1, :]))
                reached(ve, ee_ready, p)
                ve.tensor_tensor(dd[:], mx[:, :, 1:2], mx[:, :, 0:1], ALU.subtract).then_inc(diff_ready, 1)

            def mark(p):
                link(ve.tensor_copy(mif[:], mi[:, :, 0:2]))
                link(ve.tensor_tensor(oh[:], iota_e[:].unsqueeze(1).unsqueeze(1).broadcast_to([P, 2, 2, NE]),
                                      mif[:].unsqueeze(3).broadcast_to([P, 2, 2, NE]), ALU.is_equal))
                link(ve.tensor_tensor(mask[:], oh[:, :, 0, :], oh[:, :, 1, :], ALU.add))
                ve.tensor_tensor(before[:, 1, :], before[:, 0, :], mask[:, 0, :], ALU.add).then_inc(mask_ready, 1)

            def place(p):
                ve.wait_ge(ee_ready, p + 1)
                link(ve.tensor_scalar(s1[:], ee[:], 1.0, None, ALU.add))
                link(ve.reciprocal(pr[:, :, 0:1], s1[:]))
                link(ve.tensor_tensor(pr[:, :, 1:2], ee[:], pr[:, :, 0:1], ALU.mult))
                ve.wait_ge(pfx_done, p + 1)
                link(ve.tensor_tensor(pm[:], oh[:], PFX.unsqueeze(2).broadcast_to([P, 2, 2, NE]), ALU.mult))
                link(ve.tensor_reduce(pos[:], pm[:], AXX, ALU.add))
                link(ve.tensor_scalar(over[:], pos[:], float(CAP), float(4 * SLOTS), ALU.is_ge, ALU.mult))
                link(ve.scalar_tensor_tensor(slot[:], mif[:], float(CAP), pos[:], ALU.mult, ALU.add))
                reached(ve, slots_sent, 64 * p)
                link(ve.tensor_tensor(slot_i[:].rearrange("p (b k) -> p b k", b=2), slot[:], over[:], ALU.add))
                link(ve.tensor_copy(meta[:].rearrange("p (b k) a -> p b k a", b=2)[:, :, :, 0],
                                    tok_sb[:, bass.ds(2 * p, 2)].unsqueeze(2).broadcast_to([P, 2, 2])))
                link(ve.tensor_scalar(meta[:].bitcast(F32)[:, :, 1:2].rearrange("p (b k) a -> p b (k a)", b=2),
                                      pr[:], tg[:, 1:2], None, ALU.mult))
                ve.tensor_tensor(before[:, 0, :], before[:, 1, :], mask[:, 1, :], ALU.add).then_inc(slots_ready, 1)
                ve.wait_ge(slots_ready, p + 1)
                ve.tensor_copy(s1[:, 0, :], s1[:, 1, :]).then_inc(pfx_read, 1)

            def body(j, f):
                if f["att"]:
                    weigh(2 * j, 0)
                    decay_arg(2 * j + 1, 1, 16 * (j + 1))
                if f["fin"]:
                    normalise(j - 1)
                if f["ch"]:
                    choose(j - 3)
                if f["fin"]:
                    head_var(j - 1)
                if f["ch"]:
                    mark(j - 3)
                if f["fin"]:
                    scale_heads(j - 1)
                if f["att"]:
                    weigh(2 * j + 1, 1)
                if f["more"]:
                    decay_arg(2 * j + 2, 0, 16 * (j + 2))
                if f["fin"]:
                    res_var(j - 1)
                if f["ch"]:
                    place(j - 3)
                if f["fin"]:
                    norm_res(j - 1)

            consts(ve)
            ve.wait_ge(setup_pool, 5)
            for c in range(2):
                link(ve.tensor_copy(w_gc[:, c, :], w_gate[:, c, :]))
            ve.wait_ge(tanh_ready, 1)
            link(ve.tensor_scalar(normg[:], norm_sb[:], tg[:, 0:1], None, ALU.mult))
            ve.tensor_tensor(w_gc[:, 2:4, :], w_gate[:, 2:4, :], w_gate[:, 4:6, :], ALU.add).then_inc(setup_dve, 1)
            chain.restart(ve)
            for g in range(NB // GB):
                norm_group(g)
            chain.restart(ve)
            copy_gates(NB // GB - 1)
            gate_curves()
            ve.wait_ge(nme_ready, 1)
            decay_arg(0, 0, 16)
            late_consts(ve)
            run_bodies(ve, body, chain)

            ve.wait_ge(cnt_done, 1)
            link(ve.tensor_copy(cnt[:], CNT[0:1, :]))
            link(ve.tensor_tensor(blk[:], cnt[:].unsqueeze(2).broadcast_to([1, NE, 8]),
                                  blk_thr[:].unsqueeze(1).broadcast_to([1, NE, 8]), ALU.is_gt))
            link(ve.tensor_reduce(nblk[:], blk[:], AXX, ALU.add))
            link(ve.memset(ones_r[:], 1.0))
            link(ve.tensor_tensor_scan(end[:], ones_r[:], nblk[:], 0.0, ALU.mult, ALU.add))
            link(ve.tensor_tensor(start[:], end[:], nblk[:], ALU.subtract))
            link(ve.scalar_tensor_tensor(base[:], start[:], -float(P), exp_row[:], ALU.mult, ALU.add))

            def over_e(a):
                return a.unsqueeze(1).broadcast_to([1, TILES, NE])

            ti = tile_id[:].unsqueeze(2).broadcast_to([1, TILES, NE])
            link(ve.tensor_tensor(ge, ti, over_e(end[:]), ALU.is_ge))
            link(ve.tensor_tensor(gs, ti, over_e(start[:]), ALU.is_ge))
            link(ve.tensor_tensor(inr, gs, ge, ALU.subtract))
            link(ve.tensor_reduce(eidx[:], ge, AXX, ALU.add))
            link(ve.scalar_tensor_tensor(rowc, ti, float(P), over_e(base[:]), ALU.mult, ALU.add))
            link(ve.tensor_tensor(rowc, rowc, inr, ALU.mult))
            link(ve.tensor_reduce(rsum[:], rowc, AXX, ALU.add))
            link(ve.tensor_scalar(emp[:], eidx[:], float(NE), float(EMPTY_ROW), ALU.is_ge, ALU.mult))
            link(ve.tensor_tensor(sched_row[:], rsum[:], emp[:], ALU.add))
            ve.tensor_scalar(sched_e[:], eidx[:], float(NE - 1), None, ALU.min).then_inc(sched_ready, 1)
            ve.wait_ge(sched_ready, 1)

            def expert(i):
                return ve.value_load(sched_e[0:1, bass.ds(i, 1)], min_val=0, max_val=NE - 1)

            def copy_h(i):
                ve.wait_ge(l1_done, i + 1)
                reached(ve, ht_done, i)
                ve.tensor_copy(h_sb[:, 512:1024], HP[:, 1, :]).then_inc(h_dve, 1)

            def bias_h(i, e):
                ve.wait_ge(ht_done, i + 1)
                reached(ve, hT_ready, i)
                ve.tensor_tensor(hpre, HT,
                                 b1[:, bass.ds(e, 1), :].rearrange("p a m -> p (a m)").unsqueeze(2)
                                 .broadcast_to([P, KH, P]), ALU.add).then_inc(hpre_ready, 1)

            def bias_y(i, e):
                ve.wait_ge(l2_done, i + 1)
                reached(ve, y_ready, i)
                ve.tensor_tensor(yb, YP, b2[:, bass.ds(e, 1), :].rearrange("p a c -> p (a c)"),
                                 ALU.add).then_inc(yb_ready, 1)

            def tile_body(j, first):
                for u in range(UB):
                    i = UB * j + u
                    copy_h(i)
                    if not (first and u == 0):
                        bias_y(i - 1, expert(i - 1))
                    bias_h(i, expert(i))

            tile_body(0, True)
            with ve.Fori(1, TILES // UB) as j:
                tile_body(j, False)
            bias_y(TILES - 1, expert(TILES - 1))

        @block.scalar
        def _(act):
            def copy_T(g, c, n):
                act.wait_ge(t_done, 4 * g + n + 1)
                act.activation(qk_chunk(g, c), ps[:, c, :].rearrange("p (a u t) -> p a u t", a=2, u=2),
                               ACT.Copy).then_inc(qkT_ready, 1)

            def decay(b, u):
                act.wait_ge(masked, b + 1)
                act.activation(d_sb[:, u, :], d_sb[:, u, :], ACT.Exp).then_inc(d_ready, 1)

            def copy_v(b, p, u):
                reached(act, pv_done, b - 1)
                act.activation(v33[:, u, :, 0:DH], ctx_of(p, u).rearrange("p (h d) -> p h d", h=NH),
                               ACT.Copy).then_inc(v33_ready, 1)

            def copy_o(b, p, u):
                act.wait_ge(pv_done, b + 1)
                reached(act, o_used, p)
                act.activation(o_sb[:, u, :, :].rearrange("p (g h) d -> p g (h d)", g=2), O2,
                               ACT.Copy).then_inc(o_ready, 1)

            def square(p):
                act.wait_ge(hc_ready, p + 1)
                act.activation(hv[:], hc[:], ACT.Square).then_inc(sq_ready, 1)

            def copy_xfT(p):
                act.wait_ge(xf_t_done, p + 1)
                reached(act, rh_done, KH * p)
                act.activation(xfT[:].rearrange("p k t -> p (k t)"), ps[:, 4, :], ACT.Copy).then_inc(xfT_ready, 1)

            def copy_lgT(p):
                act.wait_ge(lgT_done, p + 1)
                reached(act, lg_done, p)
                act.activation(lgT[0:NE].rearrange("p b t -> p (b t)"), LGT, ACT.Identity,
                               bias=rb2_sb[:, 0:1]).then_inc(lgT_ready, 1)

            def relu(p, m):
                act.wait_ge(rh_done, KH * p + m + 1)
                reached(act, lgT_done, p)
                act.activation(hbuf[:, m, :], RH(m), ACT.Relu, bias=rb1_sb[:, m:m + 1]).then_inc(rh_ready, 1)

            def gate_exp(p):
                act.wait_ge(diff_ready, p + 1)
                act.activation(ee[:], dd[:], ACT.Exp).then_inc(ee_ready, 1)

            def body(j, f):
                att, rt = f["att"], f["rt"]

                def relus(*chunks):
                    if rt:
                        for m in chunks:
                            relu(j - 2, m)

                if att:
                    decay(2 * j, 0)
                    copy_v(2 * j, j, 0)
                if rt:
                    copy_xfT(j - 2)
                if f["ch"]:
                    copy_lgT(j - 3)
                if att:
                    decay(2 * j + 1, 1)
                    copy_v(2 * j + 1, j, 1)
                relus(0)
                if f["fin"]:
                    square(j - 1)
                relus(1)
                if att:
                    copy_o(2 * j, j, 0)
                if f["ch"]:
                    gate_exp(j - 3)
                relus(2, 3, 4, 5)
                if att:
                    copy_o(2 * j + 1, j, 1)
                relus(6, 7)

            consts(act)
            act.activation(tg[:], g2[:], ACT.Tanh).then_inc(tanh_ready, 1)
            for g in range(NB // GB):
                for n, c in enumerate((2, 3, 0, 1)):
                    copy_T(g, c, n)
            act.wait_ge(nab_ready, 1)
            act.activation(ex[:], nab[:], ACT.Exp).then_inc(ex_ready, 1)
            act.wait_ge(ex_ready, 1)
            act.activation(lp[:], ex[:], ACT.Ln, bias=1.0).then_inc(lp_ready, 1)
            act.wait_ge(fm_ready, 1)
            act.activation(nm[:].rearrange("p b (g r) -> p b r g", g=2),
                           fm[:].rearrange("p b (r g) -> p b r g", g=2), ACT.Exp, scale=-1.0).then_inc(nm_ready, 1)
            late_consts(act)
            act.wait_ge(setup_pool, 5)
            run_bodies(act, body)

            def copy_x(i):
                act.wait_ge(xt_done, i + 1)
                reached(act, l1_done, i)
                act.activation(xT.rearrange("p k t -> p (k t)"), ps[:, 5, 0:KC * P], ACT.Copy).then_inc(xT_ready, 1)

            def copy_h(i):
                act.wait_ge(l1_done, i + 1)
                reached(act, ht_done, i)
                act.activation(h_sb[:, 0:512], HP[:, 0, :], ACT.Copy).then_inc(h_act, 1)

            def relu_h(i):
                act.wait_ge(hpre_ready, i + 1)
                reached(act, l2_done, i)
                act.activation(hT.rearrange("p m t -> p (m t)"), c_sb[:], ACT.Relu).then_inc(hT_ready, 1)

            def gate_y(i, u, j):
                act.wait_ge(yb_ready, i + 1)
                act.wait_ge(metas_in[u], 16 * (j + 1))
                act.activation(y[:, u, :], yb, ACT.Copy,
                               scale=meta_s[:, u, 1:2].bitcast(F32)).then_inc(y_ready, 1)

            def tile_body(j, first, last):
                for u in range(UB):
                    i = UB * j + u
                    copy_h(i)
                    if not (last and u == UB - 1):
                        copy_x(i + 1)
                    if not (first and u == 0):
                        gate_y(i - 1, (u - 1) % UB, j if u else j - 1)
                    relu_h(i)

            copy_x(0)
            tile_body(0, True, False)
            with act.Fori(1, TILES // UB - 1) as j:
                tile_body(j, False, False)
            tile_body(TILES // UB - 1, False, True)
            gate_y(TILES - 1, UB - 1, TILES // UB - 1)

        @block.gpsimd
        def _(pool):
            pool.memset(v33[:], 1.0).then_inc(setup_pool, 1)
            pool.memset(zeros[:], 0.0).then_inc(setup_pool, 1)
            pool.memset(lgT[:], 0.0).then_inc(setup_pool, 1)
            pool.memset(before[:], 0.0).then_inc(setup_pool, 1)
            step = Count(pool_step)

            def power(dst, src, n, var_sem, rstd_sem, value):
                pool.wait_ge(var_sem, value)
                pool.tensor_tensor(dst[:, 0:n], src[:, 0:n], half[:, 0:n], ALU.pow).then_inc(rstd_sem, 1)

            def causal(b, u):
                pool_waits(pool, step, (arg_ready, b + 1))
                pool.affine_select(out=d_sb[:, u, :].rearrange("p (h s) -> p h s", h=NH),
                                   in_=d_sb[:, u, :].rearrange("p (h s) -> p h s", h=NH),
                                   pattern=[[0, NH], [1, S]], compare_op=ALU.is_ge, fill=NEG,
                                   base=0, channel_multiplier=-1).then_inc(masked, 1)

            def residual(p):
                pool.wait_ge(hn_ready, p + 1)
                reached(pool, rows_out, 32 * p)
                step.inc(pool.tensor_tensor(xr[:], hn[:].rearrange("p (b h) d -> p b (h d)", b=2),
                                            normg[:].unsqueeze(1).broadcast_to([P, 2, C]), ALU.mult))
                step.wait(pool)
                pool.tensor_tensor(xr[:], xr[:], w2[:, bass.ds(p, 1), 0:2, :].rearrange("p a b c -> p (a b) c"),
                                   ALU.add).then_inc(xr_ready, 1)

            def send_slots(p):
                pool_waits(pool, step, (slots_ready, p + 1))
                for q in range(4):
                    pool.indirect_dma_start(
                        meta_tab, bass.IndirectOffsetOnAxis(slot_i[:].bitcast(U32)[:, q:q + 1], 0),
                        meta[:, q, :], None, bounds_check=SLOTS - 1, oob_is_err=False).then_inc(slots_sent, 16)

            def body(j, f):
                if f["att"]:
                    causal(2 * j + 1, 1)
                if f["fin"]:
                    power(rs, vh, 16, var_h, rstd_h, j)
                    residual(j - 1)
                if f["more"]:
                    causal(2 * j + 2, 0)
                if f["fin"]:
                    power(rstd, vare, 2, var_r, rstd_r, j)
                if f["ch"]:
                    send_slots(j - 3)

            pool.memset(half[:], -0.5).then_inc(setup_pool, 1)
            pool.wait_ge(setup_pool, 5)
            for g in range(NB // GB):
                power(rstd, vare, GB, var_x, rstd_x, g + 1)
            pool.wait_ge(setup_dve, 1)
            pool.wait_ge(tables_init, 48)
            causal(0, 0)
            run_bodies(pool, body, step)

            pool.wait_ge(slots_sent, 16 * 4 * (NB // 2))
            pool.wait_ge(rows_out, 32 * PAIRS)

            def gather(i, u, j):
                pool_waits(pool, step, (metag_in[u], 16 * (j + 1)), (xt_done, i - 2))
                pool.indirect_dma_start(xg[:, u, :], None, xf_tab,
                                        bass.IndirectOffsetOnAxis(meta_g[:, u, 0:1].bitcast(U32), 0),
                                        bounds_check=N + P - 1, oob_is_err=True).then_inc(gathered[u], 16)

            def scatter(i, u, j):
                v, jj = (u - 1) % UB, (j if u else j - 1)
                pool_waits(pool, step, (y_ready, i + 1), (scattered[v], 16 * (jj + 1)))
                pool.indirect_dma_start(out, bass.IndirectOffsetOnAxis(meta_s[:, u, 0:1].bitcast(U32), 0),
                                        y[:, u, :], None, bounds_check=N + P - 1, oob_is_err=True,
                                        compute_op=ALU.add).then_inc(scattered[u], 16)

            def tile_body(j, first, last):
                for u in range(UB):
                    i = UB * j + u
                    if not (last and u >= UB - 2):
                        gather(i + 2, (u + 2) % UB, j + (u + 2) // UB)
                    if not (first and u == 0):
                        scatter(i - 1, (u - 1) % UB, j if u else j - 1)
                step.restart(pool)

            gather(0, 0, 0)
            gather(1, 1, 0)
            step.restart(pool)
            tile_body(0, True, False)
            with pool.Fori(1, TILES // UB - 1) as j:
                tile_body(j, False, False)
            tile_body(TILES // UB - 1, False, True)
            scatter(TILES - 1, UB - 1, TILES // UB - 1)


def run_bodies(eng, body, steps=None):
    lo, hi = FULL

    def run(j, f):
        body(j, f)
        if steps:
            steps.restart(eng)

    if steps:
        steps.restart(eng)
    for j in range(lo):
        run(j, flags(j))
    full = flags(lo)
    with eng.Fori(lo, hi - 1) as j:
        run(j, full)
    for j in range(hi - 1, BODIES):
        run(j, flags(j))


_INS = ["x", "ctx_1024", "g_xattn", "g_ffn", "wg", "gb", "L0_xattn_norm_w", "L0_ffn_rw1", "rb1t",
        "L0_ffn_rw2", "L0_ffn_rb2", "L0_ffn_ew1", "eb1t", "L0_ffn_ew2", "L0_ffn_eb2",
        "cst", "tri", "tokids", "meta_init"]


def kernel(**inputs):
    import numpy as _np
    import ml_dtypes
    import concourse.bacc as _bacc
    from concourse import mybir as _mybir
    from concourse.bass_utils import run_bass_kernel_spmd as _run

    a = {k: _np.asarray(v) for k, v in inputs.items()}
    order = [(hh % 2) * 4 + hh // 2 for hh in range(NH)]
    w = _np.concatenate([a["L0_xattn_igate_w"][order], a["L0_xattn_fgate_w"][order]])
    a["wg"] = w.reshape(2 * NH, 6, P).transpose(2, 1, 0)
    a["gb"] = _np.concatenate([a["L0_xattn_igate_b"][order], a["L0_xattn_fgate_b"][order]])
    a["rb1t"] = a["L0_ffn_rb1"].reshape(KH, P).T
    a["eb1t"] = a["L0_ffn_eb1"].reshape(NE, KH, P).transpose(2, 0, 1)
    cst = _np.zeros((P, 320), _np.float32)
    cst[:, 0:P] = _np.eye(P)
    cst[:, P:2 * P] = _np.triu(_np.ones((P, P)))
    cst[:, 256:264] = _np.arange(NE)
    cst[:, 264:272] = _np.arange(8) * P
    cst[:, 272:280] = _np.arange(NE) * CAP
    cst[:, 280:280 + TILES] = _np.arange(TILES)
    a["cst"] = cst
    tri = _np.ones((P, 2, P), _np.float32)
    tri[:, 0, :] = _np.triu(_np.ones((P, P)), 1)
    a["tri"] = tri.astype(ml_dtypes.bfloat16)
    a["tokids"] = (_np.arange(NB)[None, :] * P + _np.arange(P)[:, None]).astype(_np.int32)
    meta_init = _np.zeros((SLOTS + P, 2), _np.int32)
    meta_init[:, 0] = N + _np.arange(SLOTS + P) % P
    a["meta_init"] = meta_init

    nc = _bacc.Bacc("TRN2", target_bir_lowering=False, num_devices=1)
    arrays, args = {}, []
    for name in _INS:
        v = _np.ascontiguousarray(a[name])
        arrays[f"in_{name}_dram"] = v
        args.append(nc.dram_tensor(f"in_{name}_dram", v.shape, _mybir.dt.from_np(v.dtype), kind="ExternalInput").ap())
    out = nc.dram_tensor("out_0_dram", (N + P, C), _mybir.dt.float32, kind="ExternalOutput").ap()
    build(nc, *args, out)
    r = _run(nc, [arrays], core_ids=[0])
    return _np.asarray(r.results[0]["out_0_dram"])[0:N].reshape(NB, S, C)
```

```python
from contextlib import ExitStack

import numpy as np
import concourse.bass as bass
from concourse import mybir

ALU = mybir.AluOpType
ACT = mybir.ActivationFunctionType
AXX = mybir.AxisListType.X
F32 = mybir.dt.float32
F32R = mybir.dt.float32r
BF16 = mybir.dt.bfloat16
I32 = mybir.dt.int32
U32 = mybir.dt.uint32

P = 128
NB, S, C = 16, 128, 256
NH, DH = 8, 32
N = NB * S
H = 1024
NE, TOPK, CAP = 8, 2, 1024
KC = C // P
KH = H // P
PAIRS = NB // 2
TILES = (N * TOPK + NE * (P - 1)) // P
SLOTS = NE * CAP
EMPTY_ROW = SLOTS
UB = 3
assert TILES % UB == 0 and NB % 4 == 0 and PAIRS == NE
EPS_LN, EPS_DEN = 1e-5, 1e-6
SCALE = float(DH) ** -0.5
NEG = -1.0e30


class Count:

    def __init__(self, sem):
        self.sem, self.n = sem, 0

    def inc(self, ins):
        ins.then_inc(self.sem, 1)
        self.n += 1

    def wait(self, eng):
        if self.n:
            eng.wait_ge(self.sem, self.n)

    def restart(self, eng):
        self.wait(eng)
        eng.sem_clear(self.sem)
        self.n = 0


def reached(eng, sem, value):
    if isinstance(value, int) and value <= 0:
        return
    eng.wait_ge(sem, value)


def flags(j):
    return dict(att=j < PAIRS, fin=1 <= j <= PAIRS, rt=2 <= j <= PAIRS + 1, ch=3 <= j <= PAIRS + 2,
                more=j + 1 < PAIRS)


BODIES = PAIRS + 3
FULL = (4, PAIRS)
GB = 4


def build(nc, x, ctx_in, g_x, g_f, wg, gb, norm_w, rw1, rb1t, rw2, rb2, ew1, eb1t, ew2, eb2,
          cst, tri_in, tokids, meta_init, out):
    def dram(name, shape, dt):
        return nc.dram_tensor(name, shape, dt, kind="Internal").ap()

    m_dram = dram("m_dram", (NB, NH * S), F32)
    xf_tab = dram("xf_tab", (N + P, C), F32)
    meta_tab = dram("meta_tab", (SLOTS + P, 2), I32)

    with ExitStack() as stack:
        def sb(name, shape, dt=F32):
            return stack.enter_context(nc.sbuf_tensor(name, shape, dt))

        def sem(name):
            return stack.enter_context(nc.semaphore(name))

        ps = stack.enter_context(nc.psum_tensor("ps", [P, 8, 512], F32))

        cst_sb = sb("cst_sb", [P, 320])
        ident = cst_sb[:, 0:P]
        triu_incl = cst_sb[:, P:2 * P]
        iota_e = cst_sb[:, 256:256 + NE]
        blk_thr = cst_sb[0:1, 264:272]
        exp_row = cst_sb[0:1, 272:280]
        tile_id = cst_sb[0:1, 280:280 + TILES]
        tri = sb("tri", [P, 2, P], BF16)
        tok_sb = sb("tok_sb", [P, NB], I32)
        w_gate = sb("w_gate", [P, 6, 16])
        w_gc = sb("w_gc", [P, 4, 16])
        gate_b = sb("gate_b", [P, 16])
        norm_sb = sb("norm_sb", [P, C])
        normg = sb("normg", [P, C])
        g2 = sb("g2", [P, 2])
        tg = sb("tg", [P, 2])
        rb1_sb = sb("rb1_sb", [P, KH])
        rw2_sb = sb("rw2_sb", [P, KH, NE])
        rb2_sb = sb("rb2_sb", [NE, 1])
        b1 = sb("b1", [P, NE, KH])
        pairs = sb("pairs", [P, PAIRS, 8, C])
        w1h = sb("w1h", [P, 2, KC, H], F32R)
        w1l = sb("w1l", [P, 2, KC, H], F32R)
        w2h = sb("w2h", [P, 2, KH, C], F32R)
        w2l = sb("w2l", [P, 2, KH, C], F32R)
        zeros = sb("zeros", [P, C])

        stats = sb("stats", [P, GB, 6])
        mv = sb("mv", [P, GB, 2])
        spare = sb("spare", [P, 1])
        vare = sb("vare", [P, GB])
        rstd = sb("rstd", [P, GB])
        half = sb("half", [P, 16])
        gts = sb("gts", [P, NB, 16])
        nab = sb("nab", [P, NB, 8])
        ex = sb("ex", [P, NB, 8])
        lp = sb("lp", [P, NB, 8])
        lf = sb("lf", [P, NB, 8])
        fcum = sb("fcum", [P, NB * 8])
        a_sb = sb("a_sb", [P, NB, 8])
        m_sb = sb("m_sb", [P, P])
        fm = sb("fm", [P, NB, 8])
        nm = sb("nm", [P, NB, 8])

        m_bc = sb("m_bc", [P, 2, NH * S])
        d_sb = sb("d_sb", [P, 2, NH * S])
        c_sb = sb("c_sb", [P, NH * S])
        v33 = sb("v33", [P, 2, NH, DH + 1])
        o_sb = sb("o_sb", [P, 2, NH, DH + 1])
        nrm = sb("nrm", [P, 16])
        den = sb("den", [P, 16])
        hv = sb("hv", [P, 16, DH])
        sm = sb("sm", [P, 16])
        hc = sb("hc", [P, 16, DH])
        vs = sb("vs", [P, 16])
        vh = sb("vh", [P, 16])
        rs = sb("rs", [P, 16])
        hn = sb("hn", [P, 16, DH])
        xr = sb("xr", [P, 2, C])
        xf = sb("xf", [P, 2, C])
        rw1h, rw1l = w1h[:, 1, :, :], w1l[:, 1, :, :]
        xfTh, xfTl = (w[:, 1, 0:2, :] for w in (w2h, w2l))
        hbuf = sb("hbuf", [P, KH, 2 * P])
        lgT = sb("lgT", [P, 2, P])
        lg = sb("lg", [P, 2, NE])
        mx = sb("mx", [P, 2, 8])
        mi = sb("mi", [P, 2, 8], U32)
        mif = sb("mif", [P, 2, 2])
        dd = sb("dd", [P, 2, 1])
        ee = sb("ee", [P, 2, 1])
        s1 = sb("s1", [P, 2, 1])
        pr = sb("pr", [P, 2, 2])
        oh = sb("oh", [P, 2, 2, NE])
        mask = sb("mask", [P, 2, NE], BF16)
        before = sb("before", [P, 2, NE], BF16)
        pm = sb("pm", [P, 2, 2, NE])
        pos = sb("pos", [P, 2, 2])
        over = sb("over", [P, 2, 2])
        slot = sb("slot", [P, 2, 2])
        slot_i = sb("slot_i", [P, 4], I32)
        meta = sb("meta", [P, 4, 2], I32)
        qk = sb("qk", [P, 2, 4, P])
        xn = c_sb[:].rearrange("p (u c) -> p u c", u=GB)
        gT = d_sb[0:16].rearrange("p a n -> p (a n)").rearrange("p (g n) -> p g n", g=NB // GB)

        cnt = sb("cnt", [1, NE])
        blk = sb("blk", [1, NE, 8])
        nblk = sb("nblk", [1, NE])
        ones_r = sb("ones_r", [1, NE])
        end = sb("end", [1, NE])
        start = sb("start", [1, NE])
        base = sb("base", [1, NE])
        ge, gs, inr, rowc = (m_bc[0:1, k, q * 512:q * 512 + TILES * NE].rearrange("p (t e) -> p t e", e=NE)
                             for k, q in ((0, 0), (0, 1), (1, 0), (1, 1)))
        eidx = sb("eidx", [1, TILES])
        rsum = sb("rsum", [1, TILES])
        emp = sb("emp", [1, TILES])
        sched_row = sb("sched_row", [1, TILES], I32)
        sched_e = sb("sched_e", [1, TILES], I32)
        sched_code = sb("sched_code", [1, TILES], I32)
        after1 = sb("after1", [1, TILES])
        after2 = sb("after2", [1, TILES])

        meta_g = sb("meta_g", [P, UB, 2], I32)
        meta_s = sb("meta_s", [P, UB, 2], I32)
        w_raw = pairs[:, 0:4, :, :].rearrange("p (s l) m c -> p s l (m c)", s=2)
        work = pairs[:, 4:8, :, :].rearrange("p a m c -> p (a m c)")
        b2 = work[:, 0:NE * C].rearrange("p (e c) -> p e c", e=NE)
        xg, y = (work[:, q:q + UB * C].rearrange("p (u c) -> p u c", u=UB) for q in (NE * C, NE * C + UB * C))
        h_sb = work[:, 4096:5120]
        hpre = work[:, 5120:6144].rearrange("p (m t) -> p m t", m=KH)
        yb = work[:, 6144:6144 + C]
        xTh = sb("xTh", [P, KC, P], F32R)
        xTl = sb("xTl", [P, KC, P], F32R)
        hTh = sb("hTh", [P, KH, P], F32R)
        hTl = sb("hTl", [P, KH, P], F32R)
        S4 = ps[:, 0:4, 0:256]
        O2 = ps[:, 0:2, 256:256 + 4 * (DH + 1)]
        O4 = O2.rearrange("p g (j d) -> p g j d", j=4)
        LGT = ps[0:NE, 7, 0:2 * P]
        LGX = ps[:, 7, 2 * P:4 * P].rearrange("p (b t) -> p b t", b=2)
        LG = LGX[:, :, 0:NE]
        PFX = ps[:, 4, 0:2 * NE].rearrange("p (b e) -> p b e", b=2)
        CNT = ps[:, 4, 0:NE]
        T4 = ps[:, 4, :].rearrange("p (c t) -> p c t", c=4)
        GTS = ps[:, 6, 0:NB * 16].rearrange("p (b n) -> p b n", b=NB)
        FC = ps[:, 5, 0:P]
        AT = ps[:, 4, 0:P]
        MT = ps[:, 7, 0:P]

        def RH(m):
            return ps[:, 5 + m % 2, 0:2 * P]

        def row_of(p, m):
            return pairs[:, bass.ds(p, 1), m, :].rearrange("p a c -> p (a c)")

        def ctx_of(p, u):
            return row_of(p, 2 + u)

        def qk_of(p, u):
            return pairs[:, bass.ds(p, 1), 4 + 2 * u:6 + 2 * u, :].rearrange("p a m c -> p (a m c)")

        def qk_chunk(g, c):
            return (pairs[:, 2 * g:2 * g + 2, 4:8, :]
                    .rearrange("p a (u k) (d t) -> p a u k d t", u=2, d=2)[:, :, :, c // 2, c % 2, :])

        HP = ps[:, 0:2, :]
        HT = ps[:, 2:4, :].rearrange("p b (m t) -> p (b m) t", m=4)
        YP = ps[:, 4, 0:C]
        XT = ps[:, 5, 0:KC * P].rearrange("p (c t) -> p c t", c=KC)

        cst_in = sem("cst_in")
        late_in = sem("late_in")
        tables_init = sem("tables_init")
        raw_in = sem("raw_in")
        b2_in = sem("b2_in")
        rw1h_ready = sem("rw1h_ready")
        rw1l_ready = sem("rw1l_ready")
        w1h_ready = sem("w1h_ready")
        w1l_ready = sem("w1l_ready")
        w2h_ready = sem("w2h_ready")
        w2l_ready = sem("w2l_ready")
        x_in = [sem(f"x_in{g}") for g in range(NB // GB)]
        qk_in = [sem(f"qk_in{u}") for u in range(2)]
        ctx_in_s = [sem(f"ctx_in{g}") for g in range(NB // GB)]
        setup_dve = sem("setup_dve")
        setup_pool = sem("setup_pool")
        tanh_ready = sem("tanh_ready")
        xn_ready = sem("xn_ready")
        t_done = sem("t_done")
        qkT_ready = sem("qkT_ready")
        v33_ready = sem("v33_ready")
        gates_done = sem("gates_done")
        gT_ready = sem("gT_ready")
        gts_done = sem("gts_done")
        gts_ready = sem("gts_ready")
        nab_ready = sem("nab_ready")
        ex_ready = sem("ex_ready")
        lp_ready = sem("lp_ready")
        lf_ready = sem("lf_ready")
        f_done = sem("f_done")
        a_ready = sem("a_ready")
        at_done = sem("at_done")
        m_ready = sem("m_ready")
        m_stored = sem("m_stored")
        m_bc_in = [sem(f"m_bc_in{u}") for u in range(2)]
        mt_done = sem("mt_done")
        fm_ready = sem("fm_ready")
        nm_ready = sem("nm_ready")
        nme_ready = sem("nme_ready")
        s_done = sem("s_done")
        arg_ready = sem("arg_ready")
        masked = sem("masked")
        d_ready = sem("d_ready")
        c_ready = sem("c_ready")
        pv_done = sem("pv_done")
        o_ready = sem("o_ready")
        o_used = sem("o_used")
        hc_ready = sem("hc_ready")
        sq_ready = sem("sq_ready")
        hn_ready = sem("hn_ready")
        pool_step = sem("pool_step")
        xr_ready = sem("xr_ready")
        xf_ready = sem("xf_ready")
        rows_out = sem("rows_out")
        xf_t_done = sem("xf_t_done")
        xfT_ready = sem("xfT_ready")
        xfTl_ready = sem("xfTl_ready")
        rh_done = sem("rh_done")
        rh_ready = sem("rh_ready")
        lgT_done = sem("lgT_done")
        lgT_ready = sem("lgT_ready")
        lg_done = sem("lg_done")
        diff_ready = sem("diff_ready")
        ee_ready = sem("ee_ready")
        mask_ready = sem("mask_ready")
        pfx_done = sem("pfx_done")
        pfx_read = sem("pfx_read")
        slots_ready = sem("slots_ready")
        slots_sent = sem("slots_sent")
        cnt_done = sem("cnt_done")
        sched_ready = sem("sched_ready")
        var_x, rstd_x = sem("var_x"), sem("rstd_x")
        var_h, rstd_h = sem("var_h"), sem("rstd_h")
        var_r, rstd_r = sem("var_r"), sem("rstd_r")
        dve_step = sem("dve_step")
        act_step = sem("act_step")

        metag_in = [sem(f"metag_in{u}") for u in range(UB)]
        metas_in = [sem(f"metas_in{u}") for u in range(UB)]
        gathered = [sem(f"gathered{u}") for u in range(UB)]
        scattered = [sem(f"scattered{u}") for u in range(UB)]
        xt_done = sem("xt_done")
        xT_ready = sem("xT_ready")
        xTl_ready = sem("xTl_ready")
        l1_done = sem("l1_done")
        h_act = sem("h_act")
        h_dve = sem("h_dve")
        ht_done = sem("ht_done")
        hpre_ready = sem("hpre_ready")
        hT_ready = sem("hT_ready")
        hTl_ready = sem("hTl_ready")
        l2_done = sem("l2_done")
        yb_ready = sem("yb_ready")
        y_ready = sem("y_ready")

        N_CST, N_LATE = 6, 7
        block = stack.enter_context(nc.Block())

        def consts(eng):
            eng.wait_ge(cst_in, 16 * N_CST)

        def late_consts(eng):
            eng.wait_ge(late_in, 16 * N_LATE)

        def tile_code(eng, i):
            return eng.value_load(sched_code[0:1, bass.ds(i, 1)], min_val=0, max_val=3 * NE - 1)

        def load_weights(eng, e, place):
            for part, src in ((0, ew1), (1, ew2)):
                rows = w_raw[:, bass.ds(place, 1), part, :].rearrange("p a n -> p (a n)")
                n = (KC, KH)[part]
                eng.dma_start(rows.rearrange("p (k n) -> p k n", k=n),
                              src[bass.ds(e, 1), :, :].rearrange("a (k p) n -> p (a k) n", p=P)).then_inc(raw_in, 16)

        def raw_weights(place, part):
            return w_raw[:, bass.ds(place, 1), part, :].rearrange("p a n -> p (a n)")

        def split_weights(w, place):
            return w[:, bass.ds(place, 1), :, :].rearrange("p a k n -> p (a k n)")

        def pool_waits(pool, step, *conditions):
            step.wait(pool)
            for sm_, v in conditions:
                reached(pool, sm_, v)
            step.inc(pool.tensor_tensor(spare[:], half[:, 0:1], half[:, 0:1], ALU.add))
            pool.wait_ge(setup_pool, 4)
            for sm_, v in conditions:
                reached(pool, sm_, v)

        @block.sync
        def _(sp):
            def load_group(g):
                for p in (2 * g, 2 * g + 1):
                    for src, m, s in ((ctx_in, 2, ctx_in_s[g]), (x, 0, x_in[g])):
                        sp.dma_start(pairs[:, p, m:m + 2, :],
                                     src[2 * p:2 * p + 2, :, :].rearrange("b p c -> p b c")).then_inc(s, 16)

            load_group(0)
            for dst, src in ((cst_sb, cst), (w_gate, wg), (gate_b, gb.partition_broadcast(P)),
                             (norm_sb, norm_w.partition_broadcast(P))):
                sp.dma_start(dst[:], src).then_inc(cst_in, 16)
            sp.dma_start(g2[:, 0:1], g_x.partition_broadcast(P)).then_inc(cst_in, 16)
            sp.dma_start(g2[:, 1:2], g_f.partition_broadcast(P)).then_inc(cst_in, 16)
            for g in range(1, NB // GB):
                load_group(g)
            for dst, src in ((tok_sb, tokids), (rb1_sb, rb1t), (rw2_sb, rw2.rearrange("(m p) e -> p m e", p=P)),
                             (rb2_sb, rb2.unsqueeze(1)), (b1, eb1t), (tri, tri_in),
                             (hbuf[:].rearrange("p m t -> p (m t)").rearrange("p (k h) -> p k h", k=KC),
                              rw1.rearrange("(k p) h -> p k h", p=P))):
                sp.dma_start(dst[:], src).then_inc(late_in, 16)
            sp.dma_start(meta_tab, meta_init).then_inc(tables_init, 16)
            sp.wait_ge(setup_pool, 2)
            sp.dma_start(xf_tab[N:N + P, :], zeros[:]).then_inc(tables_init, 16)
            sp.dma_start(out[N:N + P, :], zeros[:]).then_inc(tables_init, 16)

            def load_qk(b, p, u):
                sp.dma_start(qk[:, u, :, :].rearrange("p c t -> p (c t)"), qk_of(p, u)).then_inc(qk_in[u], 16)

            def load_m(b, u):
                sp.dma_start(m_bc[:, u, :],
                             m_dram[bass.ds(b, 1), :].rearrange("a n -> (a n)").partition_broadcast(P)
                             ).then_inc(m_bc_in[u], 16)

            sp.wait_ge(m_ready, 1)
            sp.dma_start(m_dram.rearrange("b (h s) -> (b h) s", h=NH), m_sb[:]).then_inc(m_stored, 16)
            sp.wait_ge(qkT_ready, NB)
            for u in range(2):
                load_qk(u, 0, u)
            sp.wait_ge(m_stored, 16)
            for u in range(2):
                load_m(u, u)

            def body(j, f):
                if f["more"]:
                    for u in range(2):
                        sp.wait_ge(arg_ready, 2 * j + u + 1)
                        load_m(2 * j + 2 + u, u)
                        sp.wait_ge(s_done, 2 * j + u + 1)
                        load_qk(2 * j + 2 + u, j + 1, u)
                if f["fin"]:
                    p = j - 1
                    sp.wait_ge(xf_ready, p + 1)
                    sp.dma_start(out[bass.ds(p * 2 * P, 2 * P), :].rearrange("(b p) c -> p b c", p=P),
                                 xr[:]).then_inc(rows_out, 16)
                    sp.dma_start(xf_tab[bass.ds(p * 2 * P, 2 * P), :].rearrange("(b p) c -> p b c", p=P),
                                 xf[:]).then_inc(rows_out, 16)
                    if isinstance(p, int) and p in (1, PAIRS - 2):
                        if p > 1:
                            sp.wait_ge(raw_in, 32)
                        load_weights(sp, int(p > 1), int(p > 1))

            run_bodies(sp, body)
            sp.dma_start(b2.rearrange("p e c -> p (e c)"),
                         eb2.rearrange("e c -> (e c)").partition_broadcast(P)).then_inc(b2_in, 16)

            sp.wait_ge(sched_ready, 1)
            sp.wait_ge(slots_sent, 16 * 4 * (NB // 2))

            def load_meta(i, u, dst, s):
                row = sp.value_load(sched_row[0:1, bass.ds(i, 1)], min_val=0, max_val=SLOTS)
                return row, lambda: sp.dma_start(dst[:, u, :], meta_tab[bass.ds(row, P), :]).then_inc(s, 16)

            def for_gather(i, u, j):
                _, load = load_meta(i, u, meta_g, metag_in[u])
                reached(sp, gathered[u], 16 * j)
                load()

            def for_scatter(i, u, j):
                _, load = load_meta(i, u, meta_s, metas_in[u])
                reached(sp, scattered[u], 16 * j)
                load()

            def tile_body(j, last):
                for u in range(UB):
                    if not (last and u >= UB - 2):
                        for_gather(UB * j + u + 2, (u + 2) % UB, j + (u + 2) // UB)
                    for_scatter(UB * j + u, u, j)

            for_gather(0, 0, 0)
            for_gather(1, 1, 0)
            tile_body(0, False)
            with sp.Fori(1, TILES // UB - 1) as j:
                tile_body(j, False)
            tile_body(TILES // UB - 1, True)
            for u in range(UB):
                sp.wait_ge(scattered[u], 16 * (TILES // UB))
                sp.wait_ge(metas_in[u], 16 * (TILES // UB))
            sp.wait_ge(rows_out, 32 * PAIRS)

        @block.tensor
        def _(pe):
            def transposes_T(g, c):
                if c < 2:
                    pe.wait_ge(xn_ready, GB * (g + 1))
                else:
                    pe.wait_ge(ctx_in_s[g], 32)
                reached(pe, qkT_ready, 4 * (g - 1) + (c + 2) % 4 + 1)
                for u in range(GB):
                    src = xn[:, u, :] if c < 2 else pairs[:, 2 * g + u // 2, 2 + u % 2, :]
                    ins = pe.transpose(ps[:, c, u * P:(u + 1) * P], src[:, c % 2 * P:(c % 2 + 1) * P], ident[:])
                ins.then_inc(t_done, 1)

            def gates(g):
                reached(pe, gT_ready, g - 1)
                for n, c in enumerate((2, 3, 0, 1)):
                    pe.wait_ge(qkT_ready, 4 * g + n + 1)
                    ins = pe.matmul(ps[0:16, 4 + g % 2, :], w_gc[:, c, :], qk_chunk(g, c),
                                    start=(n == 0), stop=(n == 3))
                ins.then_inc(gates_done, 1)

            def gates_back(g):
                pe.wait_ge(gT_ready, g + 1)
                for u in range(GB):
                    ins = pe.transpose(GTS[:, GB * g + u, :], gT[:, g, u * P:(u + 1) * P], ident[0:16, 0:16])
                return ins

            def scores(b, p, u):
                pe.wait_ge(qk_in[u], 16 * (p + 1))
                reached(pe, o_ready, b)
                for g in range(2):
                    for r in range(4):
                        rows = slice(DH * r, DH * (r + 1))
                        ins = pe.matmul(S4[:, r, g * P:(g + 1) * P], qk[rows, u, 2 + g, :], qk[rows, u, g, :],
                                        start=True, stop=True, tile_position=(DH * r, 0))
                ins.then_inc(s_done, 1)

            def pv(b, u):
                pe.wait_ge(c_ready, b + 1)
                pe.wait_ge(v33_ready, b + 1)
                for h in range(NH):
                    hh = (h % 4) * 2 + h // 4
                    ins = pe.matmul(O4[:, h // 4, h % 4, :], c_sb[:, hh * P:(hh + 1) * P], v33[:, u, h, :],
                                    start=True, stop=True)
                ins.then_inc(pv_done, 1)

            def router_T(p):
                pe.wait_ge(xf_ready, p + 1)
                reached(pe, pfx_read, p - 1)
                for b in range(2):
                    for c in range(2):
                        ins = pe.transpose(T4[:, 2 * c + b, :], xf[:, b, c * P:(c + 1) * P], ident[:])
                ins.then_inc(xf_t_done, 1)

            def router_hidden(p, m):
                pe.wait_ge(xfTl_ready, p + 1)
                reached(pe, rh_ready, KH * p + m - 1)
                terms = [(w, t, k) for w, t in ((rw1h, xfTh), (rw1h, xfTl), (rw1l, xfTh)) for k in range(KC)]
                for n, (w, t, k) in enumerate(terms):
                    ins = pe.matmul(RH(m), w[:, k, m * P:(m + 1) * P], t[:, k, :],
                                    start=(n == 0), stop=(n == len(terms) - 1))
                ins.then_inc(rh_done, 1)

            def router_logits(p, half_of):
                if half_of == 0:
                    pe.wait_ge(rh_ready, KH * (p + 1))
                    reached(pe, mask_ready, p)
                for m in range(4 * half_of, 4 * half_of + 4):
                    ins = pe.matmul(LGT, rw2_sb[:, m, :], hbuf[:, m, :], start=(m == 0), stop=(m == KH - 1))
                if half_of:
                    ins.then_inc(lgT_done, 1)

            def logits_back(p):
                pe.wait_ge(lgT_ready, p + 1)
                for b in range(2):
                    ins = pe.transpose(LGX[:, b, :], lgT[:, b, :], ident[:])
                ins.then_inc(lg_done, 1)

            def prefix(p):
                pe.wait_ge(mask_ready, p + 1)
                for b in range(2):
                    pe.matmul(PFX[:, b, :], tri[:, 0, :], mask[:, b, :], start=True, stop=False)
                    ins = pe.matmul(PFX[:, b, :], tri[:, 1, :], before[:, b, :], start=False, stop=True)
                ins.then_inc(pfx_done, 1)

            def body(j, f):
                att, rt = f["att"], f["rt"]

                def hidden(*chunks):
                    if rt:
                        for m in chunks:
                            router_hidden(j - 2, m)

                if att:
                    scores(2 * j, j, 0)
                if f["ch"]:
                    router_logits(j - 3, 0)
                if rt:
                    router_T(j - 2)
                if f["ch"]:
                    router_logits(j - 3, 1)
                hidden(0)
                if f["ch"]:
                    logits_back(j - 3)
                hidden(1)
                if att:
                    pv(2 * j, 0)
                hidden(2, 3)
                if att:
                    scores(2 * j + 1, j, 1)
                hidden(4, 5)
                if att:
                    pv(2 * j + 1, 1)
                if f["ch"]:
                    prefix(j - 3)
                hidden(6, 7)

            consts(pe)
            pe.wait_ge(setup_dve, 1)
            for g in range(NB // GB):
                for c in (2, 3, 0, 1):
                    transposes_T(g, c)
                if g:
                    gates_back(g - 1)
                gates(g)
            gates_back(NB // GB - 1).then_inc(gts_done, 1)
            pe.wait_ge(lf_ready, 1)
            pe.matmul(FC, triu_incl[:], lf[:].rearrange("p b h -> p (b h)"), start=True, stop=True).then_inc(f_done, 1)
            pe.wait_ge(a_ready, 1)
            pe.transpose(AT, a_sb[:].rearrange("p b h -> p (b h)"), ident[:]).then_inc(at_done, 1)
            pe.wait_ge(m_ready, 1)
            pe.transpose(MT, m_sb[:], ident[:]).then_inc(mt_done, 1)
            pe.wait_ge(fm_ready, 1)
            late_consts(pe)
            pe.wait_ge(rw1h_ready, 1)
            pe.wait_ge(rw1l_ready, 1)
            run_bodies(pe, body)

            pe.wait_ge(pfx_read, NB // 2)
            pe.matmul(CNT, tri[:, 1, :], before[:, 0, :], start=True, stop=True).then_inc(cnt_done, 1)

            pe.wait_ge(sched_ready, 1)

            def x_transpose(i, u, j):
                pe.wait_ge(gathered[u], 16 * (j + 1))
                reached(pe, xTl_ready, i)
                for c in range(KC):
                    ins = pe.transpose(XT[:, c, :], xg[:, u, c * P:(c + 1) * P], ident[:])
                ins.then_inc(xt_done, 1)

            def layer1(i, code):
                pe.wait_ge(xTl_ready, i + 1)
                pe.wait_ge(w1l_ready, code % NE + 1)
                reached(pe, h_act, i)
                reached(pe, h_dve, i)
                terms = [(t, w, k) for t, w in ((xTh, w1h), (xTh, w1l), (xTl, w1h)) for k in range(KC)]
                for n in range(2):
                    for q, (t, w, k) in enumerate(terms):
                        ins = pe.matmul(HP[:, n, :], t[:, k, :],
                                        w[:, bass.ds(code % 2, 1), k, n * 512:(n + 1) * 512].rearrange("p a n -> p (a n)"),
                                        start=(q == 0), stop=(q == len(terms) - 1))
                ins.then_inc(l1_done, 1)

            def h_transpose(i):
                pe.wait_ge(h_act, i + 1)
                pe.wait_ge(h_dve, i + 1)
                reached(pe, hpre_ready, 2 * i)
                for m in range(KH):
                    ins = pe.transpose(HT[:, m, :], h_sb[:, m * P:(m + 1) * P], ident[:])
                ins.then_inc(ht_done, 1)

            def layer2(i, code):
                pe.wait_ge(w2l_ready, code % NE + 1)
                reached(pe, yb_ready, i)
                for m in range(KH):
                    if m % 4 == 0:
                        pe.wait_ge(hTl_ready, 2 * i + m // 4 + 1)
                    for t, w in ((hTh, w2h), (hTh, w2l), (hTl, w2h)):
                        first, last = m == 0 and (t, w) == (hTh, w2h), m == KH - 1 and t is hTl
                        ins = pe.matmul(YP, t[:, m, :],
                                        w[:, bass.ds(code % 2, 1), m, :].rearrange("p a n -> p (a n)"),
                                        start=first, stop=last)
                ins.then_inc(l2_done, 1)

            def tile_body(j, first, last):
                for u in range(UB):
                    i = UB * j + u
                    before_code = None if first and u == 0 else tile_code(pe, i - 1)
                    next_code = None if last and u == UB - 1 else tile_code(pe, i + 1)
                    if next_code is not None:
                        x_transpose(i + 1, (u + 1) % UB, j + (u + 1) // UB)
                    if before_code is not None:
                        layer2(i - 1, before_code)
                    h_transpose(i)
                    if next_code is not None:
                        layer1(i + 1, next_code)

            x_transpose(0, 0, 0)
            layer1(0, tile_code(pe, 0))
            tile_body(0, True, False)
            with pe.Fori(1, TILES // UB - 1) as j:
                tile_body(j, False, False)
            tile_body(TILES // UB - 1, False, True)
            layer2(TILES - 1, tile_code(pe, TILES - 1))

        @block.vector
        def _(ve):
            chain = Count(dve_step)

            def link(ins):
                chain.inc(ins)
                chain.wait(ve)

            def both(first, second):
                chain.inc(first)
                link(second)

            def norm_group(g):
                ve.wait_ge(x_in[g], 32)

                def x_of(u):
                    return pairs[:, 2 * g + u // 2, u % 2, :]

                for u in range(GB):
                    chain.inc(ve.bn_stats(stats[:, u, :], x_of(u)))
                chain.wait(ve)
                for u in range(GB):
                    chain.inc(ve.bn_aggr(mv[:, u, :], stats[:, u, :]))
                chain.wait(ve)
                ve.tensor_scalar(vare[:], mv[:, :, 1], EPS_LN, None, ALU.add).then_inc(var_x, 1)
                if g:
                    copy_gates(g - 1)
                ve.wait_ge(rstd_x, g + 1)
                reached(ve, t_done, 4 * g)
                for u in range(GB):
                    ve.tensor_scalar(xn[:, u, :], x_of(u), mv[:, u, 0:1],
                                     rstd[:, u:u + 1], ALU.subtract, ALU.mult).then_inc(xn_ready, 1)

            def copy_gates(g):
                ve.wait_ge(gates_done, g + 1)
                ve.tensor_copy(gT[:, g, :], ps[0:16, 4 + g % 2, :]).then_inc(gT_ready, 1)

            def gate_curves():
                ve.wait_ge(gts_done, 1)
                ve.tensor_tensor(gts[:], GTS, gate_b[:].unsqueeze(1).broadcast_to([P, NB, 16]),
                                 ALU.add).then_inc(gts_ready, 1)
                ve.wait_ge(gts_ready, 1)
                f_raw = gts[:, :, 8:16]
                ve.scalar_tensor_tensor(nab[:], f_raw, -1.0, f_raw, ALU.mult, ALU.min).then_inc(nab_ready, 1)
                ve.wait_ge(lp_ready, 1)
                ve.scalar_tensor_tensor(lf[:], f_raw, 0.0, lp[:], ALU.min, ALU.subtract).then_inc(lf_ready, 1)
                ve.wait_ge(f_done, 1)
                link(ve.tensor_copy(fcum[:], FC))
                ve.tensor_tensor(a_sb[:], gts[:, :, 0:8], fcum[:].rearrange("p (b h) -> p b h", b=NB),
                                 ALU.subtract).then_inc(a_ready, 1)
                ve.wait_ge(at_done, 1)
                ve.tensor_tensor_scan(m_sb[:], zeros[:, 0:P], AT, -3.0e38, ALU.add, ALU.max).then_inc(m_ready, 1)
                ve.wait_ge(mt_done, 1)
                ve.tensor_tensor(fm[:].rearrange("p b h -> p (b h)"), fcum[:], MT, ALU.add).then_inc(fm_ready, 1)
                ve.wait_ge(nm_ready, 1)
                ve.tensor_scalar(nm[:], nm[:], EPS_DEN, None, ALU.add).then_inc(nme_ready, 1)

            def decay_arg(b, u, loads):
                ve.wait_ge(m_bc_in[u], loads)
                reached(ve, c_ready, b - 1)
                ve.tensor_tensor(d_sb[:, u, :].rearrange("p (h s) -> p h s", h=NH),
                                 a_sb[:, bass.ds(b, 1), :].rearrange("p a h -> p (a h)").unsqueeze(2)
                                 .broadcast_to([P, NH, S]),
                                 m_bc[:, u, :].rearrange("p (h s) -> p h s", h=NH),
                                 ALU.subtract).then_inc(arg_ready, 1)

            def weigh(b, u):
                ve.wait_ge(s_done, b + 1)
                ve.wait_ge(d_ready, b + 1)
                reached(ve, pv_done, b)
                ve.scalar_tensor_tensor(c_sb[:].rearrange("p (r n) -> p r n", r=4), S4, SCALE,
                                        d_sb[:, u, :].rearrange("p (r n) -> p r n", r=4),
                                        ALU.mult, ALU.mult).then_inc(c_ready, 1)

            o_pair = o_sb[:].rearrange("p b h d -> p (b h) d")

            def over_d(a):
                return a.unsqueeze(2).broadcast_to([P, 16, DH])

            def rest_of_xfT(p):
                ve.wait_ge(xfT_ready, p + 1)
                ve.tensor_tensor(xfTl.rearrange("p k t -> p (k t)"), ps[:, 4, :],
                                 xfTh.rearrange("p k t -> p (k t)").bitcast(F32), ALU.subtract).then_inc(xfTl_ready, 1)

            def rest_of_weights(part, e, place):
                wh, wl, h_ready, l_ready = ((w1h, w1l, w1h_ready, w1l_ready), (w2h, w2l, w2h_ready, w2l_ready))[part]
                ve.wait_ge(h_ready, e + 1)
                ve.tensor_tensor(split_weights(wl, place), raw_weights(place, part),
                                 split_weights(wh, place).bitcast(F32), ALU.subtract).then_inc(l_ready, 1)

            def normalise(p):
                ve.wait_ge(o_ready, 2 * (p + 1))
                rowsum = o_pair[:, :, DH]
                link(ve.scalar_tensor_tensor(nrm[:], rowsum, -1.0, rowsum, ALU.mult, ALU.max))
                link(ve.scalar_tensor_tensor(nrm[:], nrm[:], EPS_DEN,
                                             nm[:, bass.ds(2 * p, 2), :].rearrange("p b h -> p (b h)"),
                                             ALU.add, ALU.max))
                link(ve.reciprocal(den[:], nrm[:]))
                ve.tensor_tensor(hv[:], o_pair[:, :, 0:DH], over_d(den[:]), ALU.mult).then_inc(o_used, 1)
                ve.wait_ge(o_used, p + 1)
                link(ve.tensor_reduce(sm[:], hv[:], AXX, ALU.add))
                ve.scalar_tensor_tensor(hc[:], over_d(sm[:]), -1.0 / DH, hv[:],
                                        ALU.mult, ALU.add).then_inc(hc_ready, 1)

            def head_var(p):
                ve.wait_ge(sq_ready, p + 1)
                link(ve.tensor_reduce(vs[:], hv[:], AXX, ALU.add))
                ve.tensor_scalar(vh[:], vs[:], 1.0 / DH, EPS_LN, ALU.mult, ALU.add).then_inc(var_h, 1)

            def scale_heads(p):
                ve.wait_ge(rstd_h, p + 1)
                reached(ve, xr_ready, p)
                ve.tensor_tensor(hn[:], hc[:], over_d(rs[:]), ALU.mult).then_inc(hn_ready, 1)

            def res_var(p):
                ve.wait_ge(xr_ready, p + 1)
                both(ve.bn_stats(stats[:, 0, :], xr[:, 0, :]), ve.bn_stats(stats[:, 1, :], xr[:, 1, :]))
                both(ve.bn_aggr(mv[:, 0, :], stats[:, 0, :]), ve.bn_aggr(mv[:, 1, :], stats[:, 1, :]))
                ve.tensor_scalar(vare[:, 0:2], mv[:, 0:2, 1], EPS_LN, None, ALU.add).then_inc(var_r, 1)

            def norm_res(p):
                ve.wait_ge(rstd_r, p + 1)
                reached(ve, rows_out, 32 * p)
                reached(ve, xf_t_done, p)
                link(ve.tensor_scalar(xf[:, 0, :], xr[:, 0, :], mv[:, 0, 0:1], rstd[:, 0:1], ALU.subtract, ALU.mult))
                ve.tensor_scalar(xf[:, 1, :], xr[:, 1, :], mv[:, 1, 0:1], rstd[:, 1:2],
                                 ALU.subtract, ALU.mult).then_inc(xf_ready, 1)

            def choose(p):
                ve.wait_ge(lg_done, p + 1)
                link(ve.tensor_copy(lg[:], LG))
                both(ve.max(mx[:, 0, :], lg[:, 0, :]), ve.max(mx[:, 1, :], lg[:, 1, :]))
                both(ve.max_index(mi[:, 0, :], mx[:, 0, :], lg[:, 0, :]),
                     ve.max_index(mi[:, 1, :], mx[:, 1, :], lg[:, 1, :]))
                reached(ve, ee_ready, p)
                ve.tensor_tensor(dd[:], mx[:, :, 1:2], mx[:, :, 0:1], ALU.subtract).then_inc(diff_ready, 1)

            def mark(p):
                link(ve.tensor_copy(mif[:], mi[:, :, 0:2]))
                link(ve.tensor_tensor(oh[:], iota_e[:].unsqueeze(1).unsqueeze(1).broadcast_to([P, 2, 2, NE]),
                                      mif[:].unsqueeze(3).broadcast_to([P, 2, 2, NE]), ALU.is_equal))
                link(ve.tensor_tensor(mask[:], oh[:, :, 0, :], oh[:, :, 1, :], ALU.add))
                ve.tensor_tensor(before[:, 1, :], before[:, 0, :], mask[:, 0, :], ALU.add).then_inc(mask_ready, 1)

            def place(p):
                ve.wait_ge(ee_ready, p + 1)
                link(ve.tensor_scalar(s1[:], ee[:], 1.0, None, ALU.add))
                link(ve.reciprocal(pr[:, :, 0:1], s1[:]))
                link(ve.tensor_tensor(pr[:, :, 1:2], ee[:], pr[:, :, 0:1], ALU.mult))
                ve.wait_ge(pfx_done, p + 1)
                link(ve.tensor_tensor(pm[:], oh[:], PFX.unsqueeze(2).broadcast_to([P, 2, 2, NE]), ALU.mult))
                link(ve.tensor_reduce(pos[:], pm[:], AXX, ALU.add))
                link(ve.tensor_scalar(over[:], pos[:], float(CAP), float(4 * SLOTS), ALU.is_ge, ALU.mult))
                link(ve.scalar_tensor_tensor(slot[:], mif[:], float(CAP), pos[:], ALU.mult, ALU.add))
                reached(ve, slots_sent, 64 * p)
                link(ve.tensor_tensor(slot_i[:].rearrange("p (b k) -> p b k", b=2), slot[:], over[:], ALU.add))
                link(ve.tensor_copy(meta[:].rearrange("p (b k) a -> p b k a", b=2)[:, :, :, 0],
                                    tok_sb[:, bass.ds(2 * p, 2)].unsqueeze(2).broadcast_to([P, 2, 2])))
                link(ve.tensor_scalar(meta[:].bitcast(F32)[:, :, 1:2].rearrange("p (b k) a -> p b (k a)", b=2),
                                      pr[:], tg[:, 1:2], None, ALU.mult))
                ve.tensor_tensor(before[:, 0, :], before[:, 1, :], mask[:, 1, :], ALU.add).then_inc(slots_ready, 1)
                ve.wait_ge(slots_ready, p + 1)
                ve.tensor_copy(s1[:, 0, :], s1[:, 1, :]).then_inc(pfx_read, 1)

            def body(j, f):
                if f["att"]:
                    weigh(2 * j, 0)
                if f["rt"]:
                    rest_of_xfT(j - 2)
                if f["att"]:
                    decay_arg(2 * j + 1, 1, 16 * (j + 1))
                if f["fin"]:
                    normalise(j - 1)
                if f["ch"]:
                    choose(j - 3)
                if f["fin"]:
                    head_var(j - 1)
                if f["ch"]:
                    mark(j - 3)
                if f["att"]:
                    weigh(2 * j + 1, 1)
                if f["fin"]:
                    scale_heads(j - 1)
                if f["more"]:
                    decay_arg(2 * j + 2, 0, 16 * (j + 2))
                if f["fin"]:
                    res_var(j - 1)
                if f["ch"]:
                    place(j - 3)
                if f["fin"]:
                    norm_res(j - 1)
                if isinstance(j, int) and j == PAIRS + 1:
                    rest_of_weights(0, 0, 0)
                    rest_of_weights(1, 0, 0)

            consts(ve)
            ve.wait_ge(setup_pool, 5)
            for c in range(2):
                link(ve.tensor_copy(w_gc[:, c, :], w_gate[:, c, :]))
            ve.wait_ge(tanh_ready, 1)
            link(ve.tensor_scalar(normg[:], norm_sb[:], tg[:, 0:1], None, ALU.mult))
            ve.tensor_tensor(w_gc[:, 2:4, :], w_gate[:, 2:4, :], w_gate[:, 4:6, :], ALU.add).then_inc(setup_dve, 1)
            chain.restart(ve)
            for g in range(NB // GB):
                norm_group(g)
            chain.restart(ve)
            copy_gates(NB // GB - 1)
            gate_curves()
            late_consts(ve)
            ve.wait_ge(rw1h_ready, 1)
            ve.tensor_tensor(rw1l.rearrange("p k h -> p (k h)"), hbuf[:].rearrange("p m t -> p (m t)"),
                             rw1h.rearrange("p k h -> p (k h)").bitcast(F32), ALU.subtract).then_inc(rw1l_ready, 1)
            ve.wait_ge(nme_ready, 1)
            decay_arg(0, 0, 16)
            run_bodies(ve, body, chain)

            ve.wait_ge(cnt_done, 1)
            link(ve.tensor_copy(cnt[:], CNT[0:1, :]))
            link(ve.tensor_tensor(blk[:], cnt[:].unsqueeze(2).broadcast_to([1, NE, 8]),
                                  blk_thr[:].unsqueeze(1).broadcast_to([1, NE, 8]), ALU.is_gt))
            link(ve.tensor_reduce(nblk[:], blk[:], AXX, ALU.add))
            link(ve.memset(ones_r[:], 1.0))
            link(ve.tensor_tensor_scan(end[:], ones_r[:], nblk[:], 0.0, ALU.mult, ALU.add))
            link(ve.tensor_tensor(start[:], end[:], nblk[:], ALU.subtract))
            link(ve.scalar_tensor_tensor(base[:], start[:], -float(P), exp_row[:], ALU.mult, ALU.add))

            def over_e(a):
                return a.unsqueeze(1).broadcast_to([1, TILES, NE])

            ti = tile_id[:].unsqueeze(2).broadcast_to([1, TILES, NE])
            link(ve.tensor_tensor(ge, ti, over_e(end[:]), ALU.is_ge))
            link(ve.tensor_tensor(gs, ti, over_e(start[:]), ALU.is_ge))
            link(ve.tensor_tensor(inr, gs, ge, ALU.subtract))
            link(ve.tensor_reduce(eidx[:], ge, AXX, ALU.add))
            link(ve.tensor_tensor(ge, ti, over_e(start[:]), ALU.is_equal))
            link(ve.tensor_reduce(after1[:], ge[:, :, 0:NE - 1], AXX, ALU.add))
            link(ve.tensor_reduce(after2[:], ge[:, :, 0:NE - 2], AXX, ALU.add))
            link(ve.tensor_tensor(after1[:], after1[:], after2[:], ALU.add))
            link(ve.scalar_tensor_tensor(rowc, ti, float(P), over_e(base[:]), ALU.mult, ALU.add))
            link(ve.tensor_tensor(rowc, rowc, inr, ALU.mult))
            link(ve.tensor_reduce(rsum[:], rowc, AXX, ALU.add))
            link(ve.tensor_scalar(emp[:], eidx[:], float(NE), float(EMPTY_ROW), ALU.is_ge, ALU.mult))
            link(ve.tensor_tensor(sched_row[:], rsum[:], emp[:], ALU.add))
            link(ve.tensor_scalar(eidx[:], eidx[:], float(NE - 1), None, ALU.min))
            link(ve.tensor_copy(sched_e[:], eidx[:]))
            ve.scalar_tensor_tensor(sched_code[:], after1[:], float(NE), eidx[:],
                                    ALU.mult, ALU.add).then_inc(sched_ready, 1)
            ve.wait_ge(sched_ready, 1)

            def copy_h(i):
                ve.wait_ge(l1_done, i + 1)
                reached(ve, ht_done, i)
                ve.tensor_copy(h_sb[:, 512:1024], HP[:, 1, :]).then_inc(h_dve, 1)

            def rest_of_x(i):
                ve.wait_ge(xT_ready, i + 1)
                ve.tensor_tensor(xTl[:].rearrange("p k t -> p (k t)"), ps[:, 5, 0:KC * P],
                                 xTh[:].rearrange("p k t -> p (k t)").bitcast(F32), ALU.subtract).then_inc(xTl_ready, 1)

            def bias_h(i, e):
                for q in range(2):
                    if q == 0:
                        ve.wait_ge(ht_done, i + 1)
                    ms = slice(4 * q, 4 * q + 4)
                    ve.tensor_tensor(hpre[:, ms, :], HT[:, ms, :],
                                     b1[:, bass.ds(e, 1), ms].rearrange("p a m -> p (a m)").unsqueeze(2)
                                     .broadcast_to([P, 4, P]), ALU.add).then_inc(hpre_ready, 1)

            def rest_of_h(i):
                for q in range(2):
                    ve.wait_ge(hT_ready, 2 * i + q + 1)
                    ms = slice(4 * q, 4 * q + 4)
                    ve.scalar_tensor_tensor(hTl[:, ms, :], hpre[:, ms, :], 0.0, hTh[:, ms, :].bitcast(F32),
                                            ALU.max, ALU.subtract).then_inc(hTl_ready, 1)

            def bias_y(i, e):
                ve.wait_ge(l2_done, i + 1)
                reached(ve, y_ready, i)
                ve.tensor_tensor(yb, YP, b2[:, bass.ds(e, 1), :].rearrange("p a c -> p (a c)"),
                                 ALU.add).then_inc(yb_ready, 1)

            def tile_body(j, first, last):
                before_code = None if first else tile_code(ve, UB * j - 1)
                for u in range(UB):
                    i = UB * j + u
                    code = tile_code(ve, i)
                    e = code % NE
                    copy_h(i)
                    if not (last and u == UB - 1):
                        rest_of_x(i + 1)
                    with ve.If(code >= NE):
                        rest_of_weights(0, e + 1, (e + 1) % 2)
                    if before_code is not None:
                        bias_y(i - 1, before_code % NE)
                    bias_h(i, e)
                    rest_of_h(i)
                    with ve.If(code >= NE):
                        rest_of_weights(1, e + 1, (e + 1) % 2)
                    before_code = code

            ve.wait_ge(b2_in, 16)
            rest_of_x(0)
            tile_body(0, True, False)
            with ve.Fori(1, TILES // UB - 1) as j:
                tile_body(j, False, False)
            tile_body(TILES // UB - 1, False, True)
            bias_y(TILES - 1, tile_code(ve, TILES - 1) % NE)

        @block.scalar
        def _(act):
            def copy_T(g, c, n):
                act.wait_ge(t_done, 4 * g + n + 1)
                act.activation(qk_chunk(g, c), ps[:, c, :].rearrange("p (a u t) -> p a u t", a=2, u=2),
                               ACT.Copy).then_inc(qkT_ready, 1)

            def decay(b, u):
                act.wait_ge(masked, b + 1)
                act.activation(d_sb[:, u, :], d_sb[:, u, :], ACT.Exp).then_inc(d_ready, 1)

            def copy_v(b, p, u):
                reached(act, pv_done, b - 1)
                act.activation(v33[:, u, :, 0:DH], ctx_of(p, u).rearrange("p (h d) -> p h d", h=NH),
                               ACT.Copy).then_inc(v33_ready, 1)

            def copy_o(b, p, u):
                act.wait_ge(pv_done, b + 1)
                reached(act, o_used, p)
                act.activation(o_sb[:, u, :, :].rearrange("p (g h) d -> p g (h d)", g=2), O2,
                               ACT.Copy).then_inc(o_ready, 1)

            def square(p):
                act.wait_ge(hc_ready, p + 1)
                act.activation(hv[:], hc[:], ACT.Square).then_inc(sq_ready, 1)

            def copy_xfT(p):
                act.wait_ge(xf_t_done, p + 1)
                reached(act, rh_done, KH * p)
                act.activation(xfTh.rearrange("p k t -> p (k t)"), ps[:, 4, :], ACT.Copy).then_inc(xfT_ready, 1)

            def copy_lgT(p):
                act.wait_ge(lgT_done, p + 1)
                reached(act, lg_done, p)
                act.activation(lgT[0:NE].rearrange("p b t -> p (b t)"), LGT, ACT.Identity,
                               bias=rb2_sb[:, 0:1]).then_inc(lgT_ready, 1)

            def relu(p, m):
                act.wait_ge(rh_done, KH * p + m + 1)
                reached(act, lgT_done, p)
                act.activation(hbuf[:, m, :], RH(m), ACT.Relu, bias=rb1_sb[:, m:m + 1]).then_inc(rh_ready, 1)

            def split_off(part, place):
                w, ready = ((w1h, w1h_ready), (w2h, w2h_ready))[part]
                act.activation(split_weights(w, place), raw_weights(place, part), ACT.Copy).then_inc(ready, 1)

            def gate_exp(p):
                act.wait_ge(diff_ready, p + 1)
                act.activation(ee[:], dd[:], ACT.Exp).then_inc(ee_ready, 1)

            def body(j, f):
                att, rt = f["att"], f["rt"]

                def relus(*chunks):
                    if rt:
                        for m in chunks:
                            relu(j - 2, m)

                if att:
                    decay(2 * j, 0)
                    copy_v(2 * j, j, 0)
                if rt:
                    copy_xfT(j - 2)
                if f["ch"]:
                    copy_lgT(j - 3)
                if att:
                    decay(2 * j + 1, 1)
                    copy_v(2 * j + 1, j, 1)
                relus(0)
                if f["fin"]:
                    square(j - 1)
                relus(1)
                if att:
                    copy_o(2 * j, j, 0)
                if f["ch"]:
                    gate_exp(j - 3)
                relus(2, 3, 4, 5)
                if att:
                    copy_o(2 * j + 1, j, 1)
                relus(6, 7)
                if isinstance(j, int) and j == PAIRS + 1:
                    act.wait_ge(raw_in, 32)
                    split_off(0, 0)
                    split_off(1, 0)

            consts(act)
            act.activation(tg[:], g2[:], ACT.Tanh).then_inc(tanh_ready, 1)
            for g in range(NB // GB):
                for n, c in enumerate((2, 3, 0, 1)):
                    copy_T(g, c, n)
            act.wait_ge(nab_ready, 1)
            act.activation(ex[:], nab[:], ACT.Exp).then_inc(ex_ready, 1)
            act.wait_ge(ex_ready, 1)
            act.activation(lp[:], ex[:], ACT.Ln, bias=1.0).then_inc(lp_ready, 1)
            act.wait_ge(fm_ready, 1)
            act.activation(nm[:].rearrange("p b (g r) -> p b r g", g=2),
                           fm[:].rearrange("p b (r g) -> p b r g", g=2), ACT.Exp, scale=-1.0).then_inc(nm_ready, 1)
            late_consts(act)
            act.activation(rw1h.rearrange("p k h -> p (k h)"), hbuf[:].rearrange("p m t -> p (m t)"),
                           ACT.Copy).then_inc(rw1h_ready, 1)
            act.wait_ge(rw1l_ready, 1)
            act.wait_ge(setup_pool, 5)
            run_bodies(act, body)

            def copy_x(i):
                act.wait_ge(xt_done, i + 1)
                reached(act, l1_done, i)
                act.activation(xTh[:].rearrange("p k t -> p (k t)"), ps[:, 5, 0:KC * P], ACT.Copy).then_inc(xT_ready, 1)

            def copy_h(i):
                act.wait_ge(l1_done, i + 1)
                reached(act, ht_done, i)
                act.activation(h_sb[:, 0:512], HP[:, 0, :], ACT.Copy).then_inc(h_act, 1)

            def relu_h(i):
                for q in range(2):
                    act.wait_ge(hpre_ready, 2 * i + q + 1)
                    if q == 0:
                        reached(act, l2_done, i)
                    ms = slice(4 * q, 4 * q + 4)
                    act.activation(hTh[:, ms, :], hpre[:, ms, :], ACT.Relu).then_inc(hT_ready, 1)

            def gate_y(i, u, j):
                act.wait_ge(yb_ready, i + 1)
                act.wait_ge(metas_in[u], 16 * (j + 1))
                act.activation(y[:, u, :], yb, ACT.Copy,
                               scale=meta_s[:, u, 1:2].bitcast(F32)).then_inc(y_ready, 1)

            def tile_body(j, first, last):
                for u in range(UB):
                    i = UB * j + u
                    code = tile_code(act, i)
                    e = code % NE
                    copy_h(i)
                    if not (last and u == UB - 1):
                        copy_x(i + 1)
                    with act.If(code >= NE):
                        act.wait_ge(raw_in, 32 * (e + 2))
                        split_off(0, (e + 1) % 2)
                    with act.If(code >= 2 * NE):
                        low_e = act.value_load(sched_e[0:1, bass.ds(i, 1)], min_val=0, max_val=NE - 3)
                        act.wait_ge(w1l_ready, e + 1)
                        act.wait_ge(w2l_ready, e + 1)
                        load_weights(act, low_e + 2, low_e % 2)
                    if not (first and u == 0):
                        gate_y(i - 1, (u - 1) % UB, j if u else j - 1)
                    relu_h(i)
                    with act.If(code >= NE):
                        split_off(1, (e + 1) % 2)

            act.wait_ge(sched_ready, 1)
            copy_x(0)
            tile_body(0, True, False)
            with act.Fori(1, TILES // UB - 1) as j:
                tile_body(j, False, False)
            tile_body(TILES // UB - 1, False, True)
            gate_y(TILES - 1, UB - 1, TILES // UB - 1)

        @block.gpsimd
        def _(pool):
            pool.memset(v33[:], 1.0).then_inc(setup_pool, 1)
            pool.memset(zeros[:], 0.0).then_inc(setup_pool, 1)
            pool.memset(lgT[:], 0.0).then_inc(setup_pool, 1)
            pool.memset(before[:], 0.0).then_inc(setup_pool, 1)
            step = Count(pool_step)

            def power(dst, src, n, var_sem, rstd_sem, value):
                pool.wait_ge(var_sem, value)
                pool.tensor_tensor(dst[:, 0:n], src[:, 0:n], half[:, 0:n], ALU.pow).then_inc(rstd_sem, 1)

            def causal(b, u):
                pool_waits(pool, step, (arg_ready, b + 1))
                pool.affine_select(out=d_sb[:, u, :].rearrange("p (h s) -> p h s", h=NH),
                                   in_=d_sb[:, u, :].rearrange("p (h s) -> p h s", h=NH),
                                   pattern=[[0, NH], [1, S]], compare_op=ALU.is_ge, fill=NEG,
                                   base=0, channel_multiplier=-1).then_inc(masked, 1)

            def residual(p):
                pool.wait_ge(hn_ready, p + 1)
                reached(pool, rows_out, 32 * p)
                step.inc(pool.tensor_tensor(xr[:], hn[:].rearrange("p (b h) d -> p b (h d)", b=2),
                                            normg[:].unsqueeze(1).broadcast_to([P, 2, C]), ALU.mult))
                step.wait(pool)
                pool.tensor_tensor(xr[:], xr[:], pairs[:, bass.ds(p, 1), 0:2, :].rearrange("p a b c -> p (a b) c"),
                                   ALU.add).then_inc(xr_ready, 1)

            def send_slots(p):
                pool_waits(pool, step, (slots_ready, p + 1))
                for q in range(4):
                    pool.indirect_dma_start(
                        meta_tab, bass.IndirectOffsetOnAxis(slot_i[:].bitcast(U32)[:, q:q + 1], 0),
                        meta[:, q, :], None, bounds_check=SLOTS - 1, oob_is_err=False).then_inc(slots_sent, 16)

            def body(j, f):
                if f["att"]:
                    causal(2 * j + 1, 1)
                if f["fin"]:
                    power(rs, vh, 16, var_h, rstd_h, j)
                    residual(j - 1)
                if f["more"]:
                    causal(2 * j + 2, 0)
                if f["fin"]:
                    power(rstd, vare, 2, var_r, rstd_r, j)
                if f["ch"]:
                    send_slots(j - 3)

            pool.memset(half[:], -0.5).then_inc(setup_pool, 1)
            pool.wait_ge(setup_pool, 5)
            for g in range(NB // GB):
                power(rstd, vare, GB, var_x, rstd_x, g + 1)
            pool.wait_ge(setup_dve, 1)
            pool.wait_ge(tables_init, 48)
            causal(0, 0)
            run_bodies(pool, body, step)

            pool.wait_ge(slots_sent, 16 * 4 * (NB // 2))
            pool.wait_ge(rows_out, 32 * PAIRS)

            def gather(i, u, j):
                pool_waits(pool, step, (metag_in[u], 16 * (j + 1)), (xt_done, i - 2))
                pool.indirect_dma_start(xg[:, u, :], None, xf_tab,
                                        bass.IndirectOffsetOnAxis(meta_g[:, u, 0:1].bitcast(U32), 0),
                                        bounds_check=N + P - 1, oob_is_err=True).then_inc(gathered[u], 16)

            def scatter(i, u, j):
                v, jj = (u - 1) % UB, (j if u else j - 1)
                pool_waits(pool, step, (y_ready, i + 1), (scattered[v], 16 * (jj + 1)))
                pool.indirect_dma_start(out, bass.IndirectOffsetOnAxis(meta_s[:, u, 0:1].bitcast(U32), 0),
                                        y[:, u, :], None, bounds_check=N + P - 1, oob_is_err=True,
                                        compute_op=ALU.add).then_inc(scattered[u], 16)

            def tile_body(j, first, last):
                for u in range(UB):
                    i = UB * j + u
                    if not (last and u >= UB - 2):
                        gather(i + 2, (u + 2) % UB, j + (u + 2) // UB)
                    if not (first and u == 0):
                        scatter(i - 1, (u - 1) % UB, j if u else j - 1)
                step.restart(pool)

            gather(0, 0, 0)
            gather(1, 1, 0)
            step.restart(pool)
            tile_body(0, True, False)
            with pool.Fori(1, TILES // UB - 1) as j:
                tile_body(j, False, False)
            tile_body(TILES // UB - 1, False, True)
            scatter(TILES - 1, UB - 1, TILES // UB - 1)


def run_bodies(eng, body, steps=None):
    lo, hi = FULL

    def run(j, f):
        body(j, f)
        if steps:
            steps.restart(eng)

    if steps:
        steps.restart(eng)
    for j in range(lo):
        run(j, flags(j))
    full = flags(lo)
    with eng.Fori(lo, hi - 1) as j:
        run(j, full)
    for j in range(hi - 1, BODIES):
        run(j, flags(j))


_INS = ["x", "ctx_1024", "g_xattn", "g_ffn", "wg", "gb", "L0_xattn_norm_w", "L0_ffn_rw1", "rb1t",
        "L0_ffn_rw2", "L0_ffn_rb2", "L0_ffn_ew1", "eb1t", "L0_ffn_ew2", "L0_ffn_eb2",
        "cst", "tri", "tokids", "meta_init"]


def kernel(**inputs):
    import numpy as _np
    import ml_dtypes
    import concourse.bacc as _bacc
    from concourse import mybir as _mybir
    from concourse.bass_utils import run_bass_kernel_spmd as _run

    a = {k: _np.asarray(v) for k, v in inputs.items()}
    order = [(hh % 2) * 4 + hh // 2 for hh in range(NH)]
    w = _np.concatenate([a["L0_xattn_igate_w"][order], a["L0_xattn_fgate_w"][order]])
    a["wg"] = w.reshape(2 * NH, 6, P).transpose(2, 1, 0)
    a["gb"] = _np.concatenate([a["L0_xattn_igate_b"][order], a["L0_xattn_fgate_b"][order]])
    a["rb1t"] = a["L0_ffn_rb1"].reshape(KH, P).T
    a["eb1t"] = a["L0_ffn_eb1"].reshape(NE, KH, P).transpose(2, 0, 1)
    cst = _np.zeros((P, 320), _np.float32)
    cst[:, 0:P] = _np.eye(P)
    cst[:, P:2 * P] = _np.triu(_np.ones((P, P)))
    cst[:, 256:264] = _np.arange(NE)
    cst[:, 264:272] = _np.arange(8) * P
    cst[:, 264] = -1
    cst[:, 272:280] = _np.arange(NE) * CAP
    cst[:, 280:280 + TILES] = _np.arange(TILES)
    a["cst"] = cst
    tri = _np.ones((P, 2, P), _np.float32)
    tri[:, 0, :] = _np.triu(_np.ones((P, P)), 1)
    a["tri"] = tri.astype(ml_dtypes.bfloat16)
    a["tokids"] = (_np.arange(NB)[None, :] * P + _np.arange(P)[:, None]).astype(_np.int32)
    meta_init = _np.zeros((SLOTS + P, 2), _np.int32)
    meta_init[:, 0] = N + _np.arange(SLOTS + P) % P
    a["meta_init"] = meta_init

    nc = _bacc.Bacc("TRN2", target_bir_lowering=False, num_devices=1)
    arrays, args = {}, []
    for name in _INS:
        v = _np.ascontiguousarray(a[name])
        arrays[f"in_{name}_dram"] = v
        args.append(nc.dram_tensor(f"in_{name}_dram", v.shape, _mybir.dt.from_np(v.dtype), kind="ExternalInput").ap())
    out = nc.dram_tensor("out_0_dram", (N + P, C), _mybir.dt.float32, kind="ExternalOutput").ap()
    build(nc, *args, out)
    r = _run(nc, [arrays], core_ids=[0])
    return _np.asarray(r.results[0]["out_0_dram"])[0:N].reshape(NB, S, C)
```
